# Optimizing a Trainium2 kernel written in Bass

```python
import numpy as np
import jax
import jax.numpy as jnp

def _softmax(x, axis=-1):
    return jax.nn.softmax(x, axis=axis)

def _gelu(x):
    return jax.nn.gelu(x, approximate=True)

def _silu(x):
    return jax.nn.silu(x)

def _sigmoid(x):
    return jax.nn.sigmoid(x)

def _layernorm(x, axis=-1, eps=1e-05):
    m = jnp.mean(x, axis=axis, keepdims=True)
    v = jnp.var(x, axis=axis, keepdims=True)
    return (x - m) / jnp.sqrt(v + eps)

def _scatter_add(tgt, idx, src, axis=0):
    return tgt.at[idx].add(src)

def _segment_sum(src, seg, n):
    return jax.ops.segment_sum(src, seg, n)
kernel_name = 'mk_decoder_postln_d1_seqx_r4_4934c6'

def setup_inputs(seed: int=0):
    np.random.seed(seed)
    _w = jnp.asarray

    def _rec_inputs():
        import jax
        import jax.numpy as jnp
        _rk = jax.random.key(seed)
        x = -0.0002928 + 1 * jax.random.normal(jax.random.fold_in(_rk, 1), (8, 112, 256), jnp.float32)
        _lenS = 112 - jax.random.randint(jax.random.fold_in(_rk, 7), (8,), 0, max(1, 112 // 4) + 1, jnp.int32)
        _lenS2 = 375 - jax.random.randint(jax.random.fold_in(_rk, 8), (8,), 0, max(1, 375 // 4) + 1, jnp.int32)
        _ctx_1024P = jax.random.normal(jax.random.fold_in(_rk, 11), (8, 16, 256), jnp.float32)
        _ctx_1024c = jax.random.dirichlet(jax.random.fold_in(_rk, 511), 0.3 * jnp.ones((16,), jnp.float32), (8, 375))
        _ctx_1024t = jnp.einsum('bsk,bkd->bsd', _ctx_1024c, _ctx_1024P)
        _ctx_1024t = _ctx_1024t * jax.lax.rsqrt(jnp.mean(jnp.square(_ctx_1024t)) + 1e-12) * 0.953939
        ctx_1024 = -1.39393e-06 + 0.999914 * (_ctx_1024t + 0.3 * jax.random.normal(jax.random.fold_in(_rk, 611), (8, 375, 256), jnp.float32))
        _validS = jnp.arange(112)[None, :] < _lenS[:, None]
        _validS2 = jnp.arange(375)[None, :] < _lenS2[:, None]
        _causal = jnp.tril(jnp.ones((112, 112), dtype=bool))
        mask_Bx1x1xS2_ik0 = jnp.where(jnp.broadcast_to(_validS2[:, None, None, :], (8, 1, 1, 375)), 0, 1).astype(jnp.int32)
        return (x, ctx_1024, mask_Bx1x1xS2_ik0)
    x, ctx_1024, mask_Bx1x1xS2_ik0 = _rec_inputs()

    def _L0_attn_setup():
        import jax, jax.numpy as jnp
        import numpy as np
        import math
        D_MODEL = 256
        NHEAD = 16
        M = 64
        D_K = D_MODEL // NHEAD
        EPS = 1e-06

        def create_orf(key, d_k, m):
            k1, k2 = jax.random.split(key)
            n_blocks = math.ceil(m / d_k)
            blocks = jax.random.normal(k1, (n_blocks, d_k, d_k), dtype=jnp.float32)
            q, _ = jnp.linalg.qr(blocks)
            scale = jnp.linalg.norm(jax.random.normal(k2, (m, d_k), dtype=jnp.float32), axis=1)
            return scale[:, None] * q.reshape(-1, d_k)[:m]

        def feature_map(x, orf):
            m, d_k = orf.shape
            proj = x @ orf.T / d_k ** 0.25
            norm = jnp.sum(x * x, axis=-1, keepdims=True) / (2.0 * math.sqrt(d_k))
            return (jnp.exp(proj - norm) + EPS) / math.sqrt(m)
        key = jax.random.key(seed)
        ks = jax.random.split(key, 10)
        s = 1.0 / math.sqrt(D_MODEL)
        inp = {'x': jax.random.normal(ks[0], (4, 1024, D_MODEL), dtype=jnp.float32)}
        names = ['q', 'k', 'v', 'o']
        for i, n in enumerate(names):
            inp[f'W{n}'] = jax.random.uniform(ks[1 + 2 * i], (D_MODEL, D_MODEL), dtype=jnp.float32, minval=-s, maxval=s)
            inp[f'b{n}'] = jax.random.uniform(ks[2 + 2 * i], (D_MODEL,), dtype=jnp.float32, minval=-s, maxval=s)
        inp['orf'] = create_orf(ks[9], D_K, M)
        return inp
    _L0_attn_all = _L0_attn_setup()
    _L0_attn_in = {k: v for k, v in _L0_attn_all.items() if k in ('Wq', 'bq', 'Wk', 'bk', 'Wv', 'bv', 'Wo', 'bo', 'orf')}
    del _L0_attn_all

    def _L0_xattn_setup():
        import jax, jax.numpy as jnp
        import numpy as np
        D_MODEL = 256
        N_HEADS = 16
        D_V = D_MODEL // N_HEADS
        key = jax.random.key(seed)
        k1, k2, k3, k4, k5, k6 = jax.random.split(key, 6)
        N, L = (2, 512)
        return {'queries': jax.random.normal(k1, (N, L, D_MODEL), jnp.float32), 'keys': jax.random.normal(k2, (N, L, D_MODEL), jnp.float32), 'values': jax.random.normal(k3, (N, L, D_MODEL), jnp.float32), 'mask': jax.random.randint(k4, (N, 1, 1, L), 0, 2).astype(jnp.int32), 'fc_w': jax.random.normal(k5, (D_MODEL, D_MODEL), jnp.float32) / np.sqrt(D_MODEL).astype(np.float32), 'fc_b': jax.random.normal(k6, (D_MODEL,), jnp.float32) * 0.01}
    _L0_xattn_all = _L0_xattn_setup()
    _L0_xattn_in = {k: v for k, v in _L0_xattn_all.items() if k in ('fc_w', 'fc_b')}
    del _L0_xattn_all

    def _L0_ffn_setup():
        import jax, jax.numpy as jnp
        import numpy as np
        E = 8
        H = 256
        D = 256
        TOP_K = 2
        key = jax.random.key(seed)
        k0, k1, k2, k3 = jax.random.split(key, 4)
        x = jax.random.normal(k0, (1, 512, H), dtype=jnp.float32)
        router_w = jax.random.normal(k1, (E, H), dtype=jnp.float32) * (1.0 / np.sqrt(H))
        up_proj = jax.random.normal(k2, (E, H, 2 * D), dtype=jnp.float32) * (1.0 / np.sqrt(H))
        down_proj = jax.random.normal(k3, (E, D, H), dtype=jnp.float32) * (1.0 / np.sqrt(D))
        return {'x': x, 'router_w': router_w, 'up_proj': up_proj, 'down_proj': down_proj}
    _L0_ffn_all = _L0_ffn_setup()
    _L0_ffn_in = {k: v for k, v in _L0_ffn_all.items() if k in ('router_w', 'up_proj', 'down_proj')}
    del _L0_ffn_all
    return {'x': x, 'ctx_1024': ctx_1024, 'mask_Bx1x1xS2_ik0': mask_Bx1x1xS2_ik0, 'L0_attn_Wq': _L0_attn_in['Wq'], 'L0_attn_bq': _L0_attn_in['bq'], 'L0_attn_Wk': _L0_attn_in['Wk'], 'L0_attn_bk': _L0_attn_in['bk'], 'L0_attn_Wv': _L0_attn_in['Wv'], 'L0_attn_bv': _L0_attn_in['bv'], 'L0_attn_Wo': _L0_attn_in['Wo'], 'L0_attn_bo': _L0_attn_in['bo'], 'L0_attn_orf': _L0_attn_in['orf'], 'L0_xattn_fc_w': _L0_xattn_in['fc_w'], 'L0_xattn_fc_b': _L0_xattn_in['fc_b'], 'L0_ffn_router_w': _L0_ffn_in['router_w'], 'L0_ffn_up_proj': _L0_ffn_in['up_proj'], 'L0_ffn_down_proj': _L0_ffn_in['down_proj']}

def reference(x, ctx_1024, mask_Bx1x1xS2_ik0, L0_attn_Wq, L0_attn_bq, L0_attn_Wk, L0_attn_bk, L0_attn_Wv, L0_attn_bv, L0_attn_Wo, L0_attn_bo, L0_attn_orf, L0_xattn_fc_w, L0_xattn_fc_b, L0_ffn_router_w, L0_ffn_up_proj, L0_ffn_down_proj):
    import jax
    import jax.numpy as jnp

    def _L0_attn_ref(x, Wq, bq, Wk, bk, Wv, bv, Wo, bo, orf):
        import jax, jax.numpy as jnp
        import numpy as np
        import math
        D_MODEL = 256
        NHEAD = 16
        M = 64
        D_K = D_MODEL // NHEAD
        EPS = 1e-06

        def create_orf(key, d_k, m):
            k1, k2 = jax.random.split(key)
            n_blocks = math.ceil(m / d_k)
            blocks = jax.random.normal(k1, (n_blocks, d_k, d_k), dtype=jnp.float32)
            q, _ = jnp.linalg.qr(blocks)
            scale = jnp.linalg.norm(jax.random.normal(k2, (m, d_k), dtype=jnp.float32), axis=1)
            return scale[:, None] * q.reshape(-1, d_k)[:m]

        def feature_map(x, orf):
            m, d_k = orf.shape
            proj = x @ orf.T / d_k ** 0.25
            norm = jnp.sum(x * x, axis=-1, keepdims=True) / (2.0 * math.sqrt(d_k))
            return (jnp.exp(proj - norm) + EPS) / math.sqrt(m)
        B, L, D = x.shape
        H, dh = (NHEAD, D // NHEAD)

        def split(y):
            return y.reshape(B, L, H, dh).transpose(0, 2, 1, 3).reshape(B * H, L, dh)
        q = feature_map(split(x @ Wq.T + bq), orf)
        k = feature_map(split(x @ Wk.T + bk), orf)
        v = split(x @ Wv.T + bv)
        kv = jnp.einsum('nlm,nld->nmd', k, v)
        ksum = jnp.sum(k, axis=1)
        buf = jnp.concatenate([kv, ksum[..., None]], axis=-1)
        out = jnp.einsum('nlm,nmd->nld', q, buf)
        out = out[..., :-1] / out[..., -1:]
        out = out.reshape(B, H, L, dh).transpose(0, 2, 1, 3).reshape(B, L, D)
        return out @ Wo.T + bo

    def _L0_xattn_ref(queries, keys, values, mask, fc_w, fc_b):
        import jax, jax.numpy as jnp
        import numpy as np
        D_MODEL = 256
        N_HEADS = 16
        D_V = D_MODEL // N_HEADS
        N, Lq, _ = queries.shape
        Lk = keys.shape[1]
        q = queries.reshape(N, Lq, N_HEADS, D_V).transpose(0, 2, 1, 3)
        k = keys.reshape(N, Lk, N_HEADS, D_V)
        v = values.reshape(N, Lk, N_HEADS, D_V)
        energy = jnp.einsum('nhqd,nkhd->nhqk', q, k)
        energy = jnp.where(mask == 0, -jnp.inf, energy)
        attn = jax.nn.softmax(energy / jnp.sqrt(jnp.float32(D_MODEL)), axis=-1)
        out = jnp.einsum('nhqk,nkhd->nqhd', attn, v).reshape(N, Lq, N_HEADS * D_V)
        return out @ fc_w.T + fc_b

    def _L0_ffn_ref(x, router_w, up_proj, down_proj):
        import jax, jax.numpy as jnp
        import numpy as np
        E = 8
        H = 256
        D = 256
        TOP_K = 2
        B, T, _ = x.shape
        xt = x.reshape(-1, H)
        N = xt.shape[0]
        logits = jnp.einsum('nh,eh->ne', xt, router_w)
        probs = jax.nn.softmax(logits, axis=-1)
        scores, expert_idx = jax.lax.top_k(probs, TOP_K)
        scores = scores / jnp.sum(scores, axis=-1, keepdims=True)
        gate = jnp.zeros((N, E), dtype=xt.dtype).at[jnp.arange(N)[:, None], expert_idx].add(scores)
        h = jnp.einsum('nh,ehd->end', xt, up_proj)
        hidden = jax.nn.silu(h[..., :D]) * h[..., D:]
        out_e = jnp.einsum('end,edh->enh', hidden, down_proj)
        out = jnp.einsum('ne,enh->nh', gate, out_e)
        return out.reshape(B, T, H)
    x = _layernorm(x + _L0_attn_ref(x, L0_attn_Wq, L0_attn_bq, L0_attn_Wk, L0_attn_bk, L0_attn_Wv, L0_attn_bv, L0_attn_Wo, L0_attn_bo, L0_attn_orf), axis=-1)
    x = _layernorm(x + _L0_xattn_ref(x, ctx_1024, ctx_1024, mask_Bx1x1xS2_ik0, L0_xattn_fc_w, L0_xattn_fc_b), axis=-1)
    x = _layernorm(x + _L0_ffn_ref(x, L0_ffn_router_w, L0_ffn_up_proj, L0_ffn_down_proj), axis=-1)
    return x

_drawn_inputs = setup_inputs


def setup_inputs(seed=0):
    import zlib

    import numpy as np

    out = dict(_drawn_inputs(seed))
    spreads = {}
    factors = {'L0_attn_bq': 15.396, 'L0_attn_bk': 25.47}
    for name, (base, spread) in spreads.items():
        noise = np.random.default_rng([zlib.crc32(name.encode()), seed]).standard_normal(out[name].shape)
        drawn = base * np.exp(spread * noise) if base else spread * noise
        out[name] = jnp.asarray(drawn.astype(out[name].dtype))
    for name, factor in factors.items():
        out[name] = (out[name] * factor).astype(out[name].dtype)
    return out
```

```python
from contextlib import ExitStack

import concourse.bass as bass
from concourse import mybir

F32 = mybir.dt.float32
F16 = mybir.dt.float16
I32 = mybir.dt.int32
U32 = mybir.dt.uint32
ACT = mybir.ActivationFunctionType
ALU = mybir.AluOpType
AX_X = mybir.AxisListType.X

B, T, D = 8, 112, 256
S2, CH = 375, 125
NC = S2 // CH
H, DH, M = 16, 16, 64
KT = D // 128
E, DE = 8, 256
PAIRS = H // 2
QUADS = H // 4
V1 = DH + 1
FEATURE_EPS = 1e-6
LN_EPS = 1e-5
SHIFT = 64.0
BIG = 60000.0

ORDER = [
    ("A", "project"), ("B", "max0"), ("C", "expert0"), ("A", "features"), ("B", "max1"),
    ("C", "expert1"), ("A", "kv"), ("B", "shift"), ("C", "expert2"), ("A", "read"),
    ("B", "quad0"), ("A", "normalize"), ("C", "expert3"), ("B", "quad1"), ("A", "turn"),
    ("C", "expert4"), ("B", "quad2"), ("A", "output"), ("C", "expert5"), ("B", "quad3"),
    ("B", "gather"), ("A", "pack"), ("B", "normalize"), ("C", "expert6"), ("B", "turn"),
    ("C", "expert7"), ("B", "output"), ("C", "finish"), ("B", "route"),
]
LAG = {"A": 0, "B": 1, "C": 2}


class Count:

    def __init__(self, nc, ctx, name, per=1):
        self.sem = ctx.enter_context(nc.semaphore(name))
        self.per = per
        nc.sync.sem_inc(self.sem, 2 * self.per)

    def at(self, b, k=None):
        return b * self.per + (2 * self.per + (self.per if k is None else k))

    def back(self, b, depth=1):
        return b * self.per + (3 - depth) * self.per


class Landing:

    def __init__(self, nc, ctx, name, n=1):
        self.rise = 16 * n
        self.sem = [ctx.enter_context(nc.semaphore(f"{name}{p}")) for p in range(2)]
        for s in self.sem:
            nc.sync.sem_inc(s, self.rise)

    def at(self, b, p):
        return (b - p) * (self.rise // 2) + 2 * self.rise

    def back(self, b, p):
        return (b - p) * (self.rise // 2) + self.rise


def build(nc, x_rows, x_cols, ctx_cols, ctx_rows, mask, w_q, w_k, w_v, w_o, w_fc, b_qk, b_v, b_o, b_fc,
          orf_rows, w_router, w_up, w_down, ident, picks, out):
    with ExitStack() as ctx:
        def sb(name, shape, dt=F32):
            return ctx.enter_context(nc.sbuf_tensor(name, shape, dt))

        def bank(name):
            return ctx.enter_context(nc.psum_tensor(name, [128, 512], F32))

        def sem(name):
            return ctx.enter_context(nc.semaphore(name))

        wqk = sb("wqk", [128, 2, KT, 4, 128])
        wv = sb("wv", [128, KT, D])
        wo = sb("wo", [128, KT, D])
        wfc = sb("wfc", [128, KT, D])
        wr = sb("wr", [128, KT, E])
        wup = sb("wup", [128, E, KT, 2 * DE])
        wdn = sb("wdn", [128, E, DE // 128, D])
        bqk = sb("bqk", [128, 2, 4])
        bv = sb("bv", [T, D])
        bo = sb("bo", [T, D])
        bfc = sb("bfc", [T, D])
        orf = sb("orf", [128, 4 * M])
        idn = sb("idn", [128, 128])
        idh = sb("idh", [128, 128], F16)
        pick = sb("pick", [128, 2 + E + 1])
        mask_i = sb("mask_i", [1, B * S2], I32)
        mask_h = sb("mask_h", [1, B * S2], F16)

        xr = sb("xr", [T, 2, D])
        xc = sb("xc", [128, 2, KT, T])
        xbo = sb("xbo", [T, D])
        qk = sb("qk", [128, 2, 4, T])
        v1 = sb("v1", [T, H, V1])
        kf = sb("kf", [T, H * M])
        qf = sb("qf", [128, 2, 4, T])
        bd = sb("bd", [128, PAIRS, 64])
        ao = sb("ao", [128, 4, T])
        rda = sb("rda", [T, H])
        an = sb("an", [T, D])
        ant = sb("ant", [128, KT, T])
        ra = sb("ra", [T, D])
        sta = sb("sta", [T, 6])
        mva = sb("mva", [T, 2])
        rsa = sb("rsa", [T, 2])
        x1 = sb("x1", [T, 2, D])
        qs = sb("qs", [T, PAIRS, 128], F16)
        qp = sb("qp", [128, 2, PAIRS, 2, T], F16)

        kc = sb("kc", [96, 2, PAIRS, S2])
        kp = sb("kp", [128, 2, PAIRS, S2], F16)
        vx = sb("vx", [CH, 2, NC, H, V1])
        x1b = sb("x1b", [T, D])
        mx = sb("mx", [T, H])
        nm = sb("nm", [T, H], F16)
        NP = 4
        pr = sb("pr", [CH, NP, 4 * T])
        bo2 = sb("bo2", [128, QUADS, T])
        rdb = sb("rdb", [T, H])
        bn = sb("bn", [T, D])
        bnt = sb("bnt", [128, KT, T])
        rb = sb("rb", [T, D])
        stb = sb("stb", [T, 6])
        mvb = sb("mvb", [T, 2])
        rsb = sb("rsb", [T, 2])
        x2 = sb("x2", [T, 2, D])
        x2t = sb("x2t", [128, 2, KT, T])
        lg = sb("lg", [T, E])
        m8 = sb("m8", [T, 8])
        i8 = sb("i8", [T, 8], U32)
        i8f = sb("i8f", [T, 2])
        nm0 = sb("nm0", [T, 1])
        ee = sb("ee", [T, 2])
        es = sb("es", [T, 1])
        er = sb("er", [T, 1])
        gg = sb("gg", [T, 2])
        g01 = sb("g01", [T, 2, E])
        gate = sb("gate", [T, 2, E])

        th = sb("th", [128, 2, 2 * T])
        w1 = sb("w1", [128, 2, 2 * T])
        hd = sb("hd", [128, 2, 2 * T])
        acc = sb("acc", [T, 2, D])
        stc = sb("stc", [T, 6])
        mvc = sb("mvc", [T, 2])
        rsc = sb("rsc", [T, 2])
        yo = sb("yo", [T, 2, D])

        pa = [bank("pa0"), bank("pa1")]
        psc = [bank("ps0"), bank("ps1")]
        ppv = bank("ppv")
        pu = [bank("pu0"), bank("pu1")]
        pd = bank("pd")

        weights_in = sem("weights_in")
        experts_in = sem("experts_in")
        mask_in = sem("mask_in")
        mask_ready = sem("mask_ready")
        ident_ready = sem("ident_ready")
        vector_presets = sem("vector_presets")
        presets = sem("presets")

        def count(name, per=1):
            return Count(nc, ctx, name, per)

        x_in, ctx_in = Landing(nc, ctx, "x_in", 2), Landing(nc, ctx, "ctx_in", 3)
        v_in, mrow_in = Landing(nc, ctx, "v_in"), Landing(nc, ctx, "mrow_in")
        y_out = Landing(nc, ctx, "y_out")
        q_mm, k_mm, v_mm = count("q_mm"), count("k_mm"), count("v_mm")
        q_ready, k_ready, v_ready = count("q_ready"), count("k_ready"), count("v_ready")
        squares = count("squares", 2)
        kf_mm, qf_mm = count("kf_mm", 2), count("qf_mm", 2)
        kf_exp, qf_exp = count("kf_exp", 2), count("qf_exp", 2)
        kf_ready, qf_ready = count("kf_ready", 2), count("qf_ready", 2)
        kv_mm, bd_ready = count("kv_mm"), count("bd_ready", 2)
        ao_mm, ao_ready = count("ao_mm"), count("ao_ready")
        aot_mm, rda_ready, an_ready = count("aot_mm"), count("rda_ready"), count("an_ready")
        ant_mm, ant_ready = count("ant_mm"), count("ant_ready")
        wo_mm, xbo_ready, ra_ready = count("wo_mm"), count("xbo_ready"), count("ra_ready")
        sta_ready, mva_ready, rsa_ready = count("sta_ready"), count("mva_ready"), count("rsa_ready", 2)
        x1_ready, qs_ready = count("x1_ready"), count("qs_ready", 2)
        qp_mm, qp_ready = count("qp_mm"), count("qp_ready", 2)
        kp_ready = count("kp_ready", 2)
        max_mm, max_ready = count("max_mm", H), count("max_ready", H)
        nm_ready, nmt_mm, nmrow_ready = count("nm_ready"), count("nmt_mm", 2), count("nmrow_ready", 2)
        s_mm, p_ready, pv_mm = count("s_mm", QUADS * NC), count("p_ready", QUADS * NC), count("pv_mm", QUADS * NC)
        bo2_ready, bot_mm = count("bo2_ready"), count("bot_mm")
        rdb_ready, bn_ready = count("rdb_ready"), count("bn_ready")
        bnt_mm, bnt_ready, fc_mm = count("bnt_mm"), count("bnt_ready"), count("fc_mm")
        x1b_ready, rb_ready, stb_ready = count("x1b_ready"), count("rb_ready"), count("stb_ready")
        mvb_ready, rsb_ready, x2_ready = count("mvb_ready"), count("rsb_ready", 2), count("x2_ready")
        x2t_mm, x2t_ready, lg_mm, lg_ready = count("x2t_mm"), count("x2t_ready"), count("lg_mm"), count("lg_ready")
        route = count("route", 8)
        ee_ready, gate_ready = count("ee_ready"), count("gate_ready")
        up_mm, th_ready, w1_ready, hd_ready = (count(n, E) for n in ("up_mm", "th_ready", "w1_ready", "hd_ready"))
        dn_mm, acc_ready = count("dn_mm", E), count("acc_ready", E)
        stc_ready, mvc_ready, rsc_ready = count("stc_ready"), count("mvc_ready"), count("rsc_ready", 2)
        y_ready = count("y_ready")

        waited = sem("waited")

        def hold(eng, sem_, value):
            eng.wait_ge(sem_, value)
            eng.sem_inc(waited, 1)

        PRESETS = 5

        block = ctx.enter_context(nc.Block())

        def iteration(steps, i, half, stages):
            for stage, step in ORDER:
                if stage in stages and (stage, step) in steps:
                    steps[stage, step](i - LAG[stage], (half - LAG[stage]) % 2)

        def pipeline(eng, steps):
            iteration(steps, 0, 0, "A")
            iteration(steps, 1, 1, "AB")
            with eng.Fori(2, B - 1, 2) as i:
                iteration(steps, i, 0, "ABC")
                iteration(steps, i + 1, 1, "ABC")
            iteration(steps, B, B % 2, "BC")
            iteration(steps, B + 1, (B + 1) % 2, "C")

        @block.sync
        def _(sp):
            def load(b, p):
                sp.wait_ge(xbo_ready.sem, xbo_ready.back(b, 2))
                sp.wait_ge(v_mm.sem, v_mm.back(b, 2))
                sp.wait_ge(k_mm.sem, k_mm.back(b, 2))
                sp.dma_start(xc[:, p], x_cols[bass.ds(b, 1)].rearrange("o p k t -> (o p) k t")).then_inc(x_in.sem[p], 16)
                sp.dma_start(xr[:, p, :], x_rows[bass.ds(b, 1)].rearrange("o t d -> (o t) d")).then_inc(x_in.sem[p], 16)
                sp.wait_ge(kp_ready.sem, kp_ready.back(b, 2))
                for r in range(3):
                    sp.dma_start(kc[32 * r:32 * r + 32, p], ctx_cols[bass.ds(b, 1)].rearrange("o r g s -> (o r) g s")).then_inc(ctx_in.sem[p], 16)
                sp.wait_ge(pv_mm.sem, pv_mm.back(b, 2))
                sp.dma_start(vx[:, p], ctx_rows[bass.ds(b, 1)].rearrange("o s c h v -> (o s) c h v")).then_inc(v_in.sem[p], 16)
                sp.wait_ge(s_mm.sem, s_mm.back(b, 2))
                sp.dma_start(kp[97:98, p], mask_h[0:1, bass.ds(b * S2, S2)].rearrange("o (u s) -> o u s", u=1).to_broadcast([1, PAIRS, S2])).then_inc(mrow_in.sem[p], 16)

            for dst, src in ((wqk[:, 0], w_q), (wqk[:, 1], w_k), (bqk[:], b_qk), (wv[:], w_v), (orf[:], orf_rows),
                             (bv[:], b_v), (idn[:], ident), (pick[:], picks), (bo[:], b_o), (wo[:], w_o),
                             (wfc[:], w_fc), (bfc[:], b_fc), (wr[:], w_router)):
                sp.dma_start(dst, src).then_inc(weights_in, 16)
            sp.dma_start(mask_i[:], mask).then_inc(mask_in, 16)
            sp.wait_ge(mask_ready, 1)
            sp.wait_ge(presets, PRESETS)
            load(0, 0)
            load(1, 1)
            sp.dma_start(wup[:], w_up).then_inc(experts_in, 16)
            sp.dma_start(wdn[:], w_down).then_inc(experts_in, 16)
            with sp.Fori(2, B - 1, 2) as b:
                load(b, 0)
                load(b + 1, 1)
            for b in (B - 2, B - 1):
                sp.wait_ge(y_out.sem[b % 2], y_out.at(b, b % 2))

        WEIGHTS = 13 * 16

        @block.tensor
        def _(pe):
            def a_project(b, p):
                pe.wait_ge(x_in.sem[p], x_in.at(b, p))
                for n, done in ((0, q_mm), (1, k_mm)):
                    if n == 0:
                        pe.wait_ge(qp_ready.sem, qp_ready.back(b))
                    else:
                        pe.wait_ge(ra_ready.sem, ra_ready.back(b))
                    for t in range(4):
                        for k in range(KT):
                            mm = nc.tensor.matmul(pa[n][:, t * T:(t + 1) * T], wqk[:, n, k, t], xc[:, p, k],
                                                  start=(k == 0), stop=(k == KT - 1))
                    mm.then_inc(done.sem, 1)
                pe.wait_ge(q_ready.sem, q_ready.at(b))
                for k in range(KT):
                    mm = nc.tensor.matmul(pa[0][0:T, 0:D], xc[:, p, k], wv[:, k], start=(k == 0), stop=(k == KT - 1))
                mm.then_inc(v_mm.sem, 1)

            def a_features(b, p):
                pe.wait_ge(squares.sem, squares.at(b))
                for i, (free, bk) in enumerate(((k_ready, 1), (v_ready, 0))):
                    pe.wait_ge(free.sem, free.at(b))
                    for t in (2 * i, 2 * i + 1):
                        mm = nc.tensor.matmul(pa[bk][0:T, (t % 2) * 256:(t % 2) * 256 + 256], qk[:, 1, t], orf[:],
                                              start=True, stop=True)
                    mm.then_inc(kf_mm.sem, 1)
                for u in range(2):
                    pe.wait_ge(kf_exp.sem, kf_exp.at(b, u + 1))
                    mm = nc.tensor.matmul(pa[1 - u][:, 0:4 * T], orf[:, u * 128:u * 128 + 128],
                                          qk[:, 0].rearrange("p t n -> p (t n)"), start=True, stop=True)
                    mm.then_inc(qf_mm.sem, 1)

            def a_kv(b, p):
                pe.wait_ge(kf_ready.sem, kf_ready.at(b))
                pe.wait_ge(v_ready.sem, v_ready.at(b))
                pe.wait_ge(qf_exp.sem, qf_exp.at(b, 1))
                for j in range(PAIRS):
                    mm = nc.tensor.matmul(pa[1][:, j * 2 * V1:(j + 1) * 2 * V1], kf[:, j * 128:j * 128 + 128],
                                          v1[:, 2 * j:2 * j + 2].rearrange("p h d -> p (h d)"), start=True, stop=True)
                mm.then_inc(kv_mm.sem, 1)

            def a_read(b, p):
                pe.wait_ge(bd_ready.sem, bd_ready.at(b))
                pe.wait_ge(qf_ready.sem, qf_ready.at(b))
                for j in range(PAIRS):
                    r, c = 64 * (j % 2), j // 2
                    mm = nc.tensor.matmul(pa[0][r:r + 64, c * T:(c + 1) * T], bd[:, j], qf[:, j % 2, j // 2],
                                          start=True, stop=True)
                mm.then_inc(ao_mm.sem, 1)

            def a_normalize(b, p):
                pe.wait_ge(ao_ready.sem, ao_ready.at(b))
                pe.wait_ge(bd_ready.sem, bd_ready.at(b))
                for c in range(4):
                    mm = nc.tensor.transpose(pa[1][0:T, c * 128:c * 128 + 128], ao[:, c], idn[:])
                mm.then_inc(aot_mm.sem, 1)

            def a_turn(b, p):
                pe.wait_ge(an_ready.sem, an_ready.at(b))
                for k in range(KT):
                    mm = nc.tensor.transpose(pa[0][:, k * T:(k + 1) * T], an[:, k * 128:k * 128 + 128], idn[0:T, 0:T])
                mm.then_inc(ant_mm.sem, 1)

            def a_output(b, p):
                pe.wait_ge(ant_ready.sem, ant_ready.at(b))
                for k in range(KT):
                    mm = nc.tensor.matmul(pa[1][0:T, 0:D], ant[:, k], wo[:, k], start=(k == 0), stop=(k == KT - 1))
                mm.then_inc(wo_mm.sem, 1)

            def a_pack(b, p):
                pe.wait_ge(qs_ready.sem, qs_ready.at(b))
                dst = pa[0][:, 0:PAIRS * T // 2].bitcast(F16)
                for g in range(PAIRS):
                    mm = nc.tensor.transpose(dst[:, g * T:(g + 1) * T], qs[:, g], idh[0:T, 0:T])
                mm.then_inc(qp_mm.sem, 1)

            def b_max(half):
                def step(b, p):
                    if half == 0:
                        pe.wait_ge(qp_ready.sem, qp_ready.at(b))
                        pe.wait_ge(kp_ready.sem, kp_ready.at(b))
                        pe.wait_ge(mrow_in.sem[p], mrow_in.at(b, p))
                    for h in range(8 * half, 8 * half + 8):
                        if h == 0:
                            pe.wait_ge(lg_ready.sem, lg_ready.back(b))
                        elif h == 1:
                            pe.wait_ge(x2t_ready.sem, x2t_ready.back(b))
                        else:
                            pe.wait_ge(max_ready.sem, max_ready.at(b, h - 1))
                        nc.tensor.matmul(psc[h % 2][0:T, 0:S2], qp[:, p, h // 2, h % 2], kp[:, p, h // 2],
                                         start=True, stop=True).then_inc(max_mm.sem, 1)
                return step

            def b_shift(b, p):
                pe.wait_ge(nm_ready.sem, nm_ready.at(b))
                for n in range(2):
                    dst = psc[n][:, 0:8 * T // 2].bitcast(F16)
                    for h in range(8):
                        mm = nc.tensor.transpose(dst[96:97, h * T:(h + 1) * T], nm[:, 8 * n + h:8 * n + h + 1],
                                                 idh[0:T, 0:T], tile_position=(0, 96))
                    mm.then_inc(nmt_mm.sem, 1)

            def values(b, p, u):
                q, c = u // NC, u % NC
                pe.wait_ge(p_ready.sem, p_ready.at(b, u + 1))
                if u == 0:
                    pe.wait_ge(v_in.sem[p], v_in.at(b, p))
                    pe.wait_ge(bo2_ready.sem, bo2_ready.back(b))
                for j in range(4):
                    mm = nc.tensor.matmul(ppv[32 * j:32 * j + V1, q * T:(q + 1) * T], vx[:, p, c, 4 * q + j],
                                          pr[:, u % NP, j * T:(j + 1) * T], start=(c == 0), stop=(c == NC - 1))
                mm.then_inc(pv_mm.sem, 1)

            def b_quad(q):
                def step(b, p):
                    for c in range(NC):
                        u = q * NC + c
                        if u < 2:
                            pe.wait_ge(nmrow_ready.sem, nmrow_ready.at(b))
                        else:
                            pe.wait_ge(p_ready.sem, p_ready.at(b, u - 1))
                        for n in range(2):
                            mm = nc.tensor.matmul(psc[u % 2][0:CH, n * 2 * T:(n + 1) * 2 * T],
                                                  kp[:, p, 2 * q + n, c * CH:(c + 1) * CH],
                                                  qp[:, p, 2 * q + n].rearrange("p h t -> p (h t)"), start=True, stop=True)
                        mm.then_inc(s_mm.sem, 1)
                        if u >= 1:
                            values(b, p, u - 1)
                return step

            def b_gather(b, p):
                values(b, p, QUADS * NC - 1)

            def b_normalize(b, p):
                pe.wait_ge(bo2_ready.sem, bo2_ready.at(b))
                for c in range(4):
                    mm = nc.tensor.transpose(psc[0][0:T, c * 128:c * 128 + 128], bo2[:, c], idn[:])
                mm.then_inc(bot_mm.sem, 1)

            def b_turn(b, p):
                pe.wait_ge(bn_ready.sem, bn_ready.at(b))
                for k in range(KT):
                    mm = nc.tensor.transpose(psc[1][:, k * T:(k + 1) * T], bn[:, k * 128:k * 128 + 128], idn[0:T, 0:T])
                mm.then_inc(bnt_mm.sem, 1)

            def b_output(b, p):
                pe.wait_ge(bnt_ready.sem, bnt_ready.at(b))
                for k in range(KT):
                    mm = nc.tensor.matmul(psc[0][0:T, 0:D], bnt[:, k], wfc[:, k], start=(k == 0), stop=(k == KT - 1))
                mm.then_inc(fc_mm.sem, 1)

            def b_route(b, p):
                pe.wait_ge(x2_ready.sem, x2_ready.at(b))
                for k in range(KT):
                    mm = nc.tensor.transpose(psc[1][:, k * T:(k + 1) * T], x2[:, p, k * 128:k * 128 + 128], idn[0:T, 0:T])
                mm.then_inc(x2t_mm.sem, 1)
                pe.wait_ge(x2t_ready.sem, x2t_ready.at(b))
                for k in range(KT):
                    mm = nc.tensor.matmul(psc[0][0:T, 0:E], x2t[:, p, k], wr[:, k], start=(k == 0), stop=(k == KT - 1))
                mm.then_inc(lg_mm.sem, 1)

            def down(b, p, e):
                pe.wait_ge(hd_ready.sem, hd_ready.at(b, e + 1))
                if e == 0:
                    pe.wait_ge(acc_ready.sem, acc_ready.back(b))
                else:
                    pe.wait_ge(acc_ready.sem, acc_ready.at(b, e))
                for k in range(2):
                    mm = nc.tensor.matmul(pd[0:T, 0:D], hd[:, e % 2, k * T:(k + 1) * T], wdn[:, e, k],
                                          start=(k == 0), stop=(k == 1))
                mm.then_inc(dn_mm.sem, 1)

            def c_expert(e):
                def step(b, p):
                    if e == 0:
                        pe.wait_ge(x2t_ready.sem, x2t_ready.at(b))
                    if e >= 2:
                        pe.wait_ge(hd_ready.sem, hd_ready.at(b, e - 1))
                    else:
                        pe.wait_ge(hd_ready.sem, hd_ready.back(b))
                    for m in range(4):
                        for k in range(KT):
                            mm = nc.tensor.matmul(pu[e % 2][:, m * T:(m + 1) * T], wup[:, e, k, m * 128:m * 128 + 128],
                                                  x2t[:, p, k], start=(k == 0), stop=(k == KT - 1))
                    mm.then_inc(up_mm.sem, 1)
                    if e >= 1:
                        down(b, p, e - 1)
                return step

            def c_finish(b, p):
                down(b, p, E - 1)

            pe.wait_ge(weights_in, WEIGHTS)
            pe.wait_ge(experts_in, 32)
            pe.wait_ge(presets, PRESETS)
            pe.wait_ge(vector_presets, 2)
            pe.wait_ge(ident_ready, 1)
            pipeline(pe, {
                ("A", "project"): a_project, ("A", "features"): a_features, ("A", "kv"): a_kv, ("A", "read"): a_read,
                ("A", "normalize"): a_normalize, ("A", "turn"): a_turn, ("A", "output"): a_output, ("A", "pack"): a_pack,
                ("B", "max0"): b_max(0), ("B", "max1"): b_max(1), ("B", "shift"): b_shift, ("B", "gather"): b_gather,
                ("B", "normalize"): b_normalize, ("B", "turn"): b_turn, ("B", "output"): b_output, ("B", "route"): b_route,
                ("C", "finish"): c_finish,
            } | {("B", f"quad{q}"): b_quad(q) for q in range(QUADS)} | {("C", f"expert{e}"): c_expert(e) for e in range(E)})

        @block.scalar
        def _(act):
            def a_features(b, p):
                for i in range(2):
                    act.wait_ge(kf_mm.sem, kf_mm.at(b, i + 1))
                    act.wait_ge(kv_mm.sem, kv_mm.back(b))
                    nc.scalar.activation(kf[:, i * 512:i * 512 + 512], pa[1 - i][0:T, 0:512], ACT.Exp,
                                         scale=0.5).then_inc(kf_exp.sem, 1)
                for u in range(2):
                    act.wait_ge(qf_mm.sem, qf_mm.at(b, u + 1))
                    act.wait_ge(ao_mm.sem, ao_mm.back(b))
                    nc.scalar.activation(qf[:, u].rearrange("p t n -> p (t n)"), pa[1 - u][:, 0:4 * T], ACT.Exp,
                                         scale=0.5).then_inc(qf_exp.sem, 1)

            def a_kv(b, p):
                act.wait_ge(kv_mm.sem, kv_mm.at(b))
                act.wait_ge(ao_mm.sem, ao_mm.back(b))
                kv = pa[1][:, 0:PAIRS * 2 * V1].rearrange("p (j d) -> p j d", d=2 * V1)
                nc.scalar.copy(bd[0:64, :, 0:V1], kv[0:64, :, 0:V1]).then_inc(bd_ready.sem, 1)
                nc.scalar.copy(bd[64:128, :, V1:2 * V1], kv[64:128, :, V1:2 * V1]).then_inc(bd_ready.sem, 1)

            def a_read(b, p):
                act.wait_ge(ao_mm.sem, ao_mm.at(b))
                act.wait_ge(aot_mm.sem, aot_mm.back(b))
                nc.scalar.copy(ao[:].rearrange("p c t -> p (c t)"), pa[0][:, 0:4 * T]).then_inc(ao_ready.sem, 1)

            def a_turn(b, p):
                act.wait_ge(ant_mm.sem, ant_mm.at(b))
                act.wait_ge(wo_mm.sem, wo_mm.back(b))
                nc.scalar.copy(ant[:].rearrange("p k t -> p (k t)"), pa[0][:, 0:KT * T]).then_inc(ant_ready.sem, 1)

            def b_shift(b, p):
                for n in range(2):
                    act.wait_ge(nmt_mm.sem, nmt_mm.at(b, n + 1))
                    src = psc[n][:, 0:8 * T // 2].bitcast(F16)
                    nc.scalar.copy(qp[96:97, p, 4 * n:4 * n + 4].rearrange("p g h t -> p (g h t)"),
                                   src[96:97, 0:8 * T]).then_inc(nmrow_ready.sem, 1)

            def b_quad(q):
                def step(b, p):
                    for c in range(NC):
                        u = q * NC + c
                        act.wait_ge(s_mm.sem, s_mm.at(b, u + 1))
                        if u >= NP:
                            act.wait_ge(pv_mm.sem, pv_mm.at(b, u - NP + 1))
                        else:
                            act.wait_ge(pv_mm.sem, pv_mm.back(b))
                        nc.scalar.activation(pr[:, u % NP], psc[u % 2][0:CH, 0:4 * T], ACT.Exp,
                                             scale=1.0 / 16.0).then_inc(p_ready.sem, 1)
                return step

            def b_gather(b, p):
                act.wait_ge(pv_mm.sem, pv_mm.at(b))
                act.wait_ge(bot_mm.sem, bot_mm.back(b))
                nc.scalar.copy(bo2[:].rearrange("p c t -> p (c t)"), ppv[:, 0:4 * T]).then_inc(bo2_ready.sem, 1)

            def b_turn(b, p):
                act.wait_ge(bnt_mm.sem, bnt_mm.at(b))
                act.wait_ge(fc_mm.sem, fc_mm.back(b))
                nc.scalar.copy(bnt[:].rearrange("p k t -> p (k t)"), psc[1][:, 0:KT * T]).then_inc(bnt_ready.sem, 1)

            def b_route(b, p):
                act.wait_ge(x2t_mm.sem, x2t_mm.at(b))
                act.wait_ge(up_mm.sem, up_mm.back(b, 2))
                nc.scalar.copy(x2t[:, p].rearrange("p k t -> p (k t)"), psc[1][:, 0:KT * T]).then_inc(x2t_ready.sem, 1)
                act.wait_ge(route.sem, route.at(b, 2))
                nc.scalar.activation(ee[:], m8[:, 0:2], ACT.Exp, bias=nm0[:, 0:1]).then_inc(ee_ready.sem, 1)

            def c_expert(e):
                def step(b, p):
                    act.wait_ge(up_mm.sem, up_mm.at(b, e + 1))
                    if e >= 2:
                        act.wait_ge(w1_ready.sem, w1_ready.at(b, e - 1))
                    else:
                        act.wait_ge(w1_ready.sem, w1_ready.back(b))
                    nc.scalar.activation(th[:, e % 2], pu[e % 2][:, 0:2 * T], ACT.Tanh, scale=0.5).then_inc(th_ready.sem, 1)
                return step

            def c_finish(b, p):
                act.wait_ge(y_ready.sem, y_ready.at(b))
                act.dma_start(out[bass.ds(b, 1)].rearrange("o t d -> (o t) d"), yo[:, p]).then_inc(y_out.sem[p], 16)

            act.wait_ge(weights_in, WEIGHTS)
            act.wait_ge(presets, PRESETS)
            pipeline(act, {
                ("A", "features"): a_features, ("A", "kv"): a_kv, ("A", "read"): a_read, ("A", "turn"): a_turn,
                ("B", "shift"): b_shift, ("B", "gather"): b_gather, ("B", "turn"): b_turn, ("B", "route"): b_route,
                ("C", "finish"): c_finish,
            } | {("B", f"quad{q}"): b_quad(q) for q in range(QUADS)} | {("C", f"expert{e}"): c_expert(e) for e in range(E)})

        @block.vector
        def _(dve):
            def normalized(b, src, stats, mean_var, rs, st, mv, rsr, dst, done):
                nc.vector.bn_stats(stats[:], src).then_inc(st.sem, 1)
                hold(dve, st.sem, st.at(b))
                nc.vector.bn_aggr(mean_var[:], stats[:]).then_inc(mv.sem, 1)
                dve.wait_ge(rsr.sem, rsr.at(b))
                nc.vector.tensor_scalar(dst, src, mean_var[:, 0:1], rs[:, 1:2], ALU.subtract, ALU.mult).then_inc(done.sem, 1)

            def a_project(b, p):
                for n, mm, ready in ((0, q_mm, q_ready), (1, k_mm, k_ready)):
                    dve.wait_ge(mm.sem, mm.at(b))
                    used = (qf_mm, kf_mm)[n]
                    dve.wait_ge(used.sem, used.back(b))
                    nc.vector.tensor_tensor(qk[:, n], pa[n][:, 0:4 * T].rearrange("p (c t) -> p c t", c=4),
                                            bqk[:, n].unsqueeze(2).to_broadcast([128, 4, T]), ALU.add).then_inc(ready.sem, 1)
                dve.wait_ge(v_mm.sem, v_mm.at(b))
                dve.wait_ge(kv_mm.sem, kv_mm.back(b))
                nc.vector.tensor_tensor(v1[:, :, 0:DH], pa[0][0:T, 0:D].rearrange("p (h d) -> p h d", h=H),
                                        bv[:].rearrange("p (h d) -> p h d", h=H), ALU.add).then_inc(v_ready.sem, 1)

            def a_normalize(b, p):
                dve.wait_ge(aot_mm.sem, aot_mm.at(b))
                sums = pa[1][0:T, 0:512].rearrange("p (j r) -> p j r", j=PAIRS)[:, :, 0:2 * V1].rearrange(
                    "p j (h d) -> p j h d", h=2)
                nc.vector.reciprocal(rda[:].rearrange("p (j h) -> p j h", h=2), sums[:, :, :, DH]).then_inc(rda_ready.sem, 1)
                dve.wait_ge(rda_ready.sem, rda_ready.at(b))
                dve.wait_ge(ant_mm.sem, ant_mm.back(b))
                nc.vector.tensor_tensor(an[:].rearrange("p (j h d) -> p j h d", j=PAIRS, h=2), sums[:, :, :, 0:DH],
                                        rda[:].rearrange("p (j h) -> p j h", h=2).unsqueeze(3).to_broadcast([T, PAIRS, 2, DH]),
                                        ALU.mult).then_inc(an_ready.sem, 1)

            def a_output(b, p):
                dve.wait_ge(wo_mm.sem, wo_mm.at(b))
                dve.wait_ge(xbo_ready.sem, xbo_ready.at(b))
                nc.vector.tensor_tensor(ra[:], pa[1][0:T, 0:D], xbo[:], ALU.add).then_inc(ra_ready.sem, 1)
                dve.wait_ge(ra_ready.sem, ra_ready.at(b))
                normalized(b, ra[:], sta, mva, rsa, sta_ready, mva_ready, rsa_ready, x1[:, p], x1_ready)
                x1_v = x1[:, p].rearrange("p (g r) -> p g r", g=PAIRS)
                dve.wait_ge(x1_ready.sem, x1_ready.at(b))
                dve.wait_ge(qp_mm.sem, qp_mm.back(b))
                nc.vector.tensor_copy(
                    qs[:, :, 0:128].rearrange("p g (n r) -> p g n r", n=2)[:, :, :, 0:32],
                    x1_v.unsqueeze(2).to_broadcast([T, PAIRS, 2, 32])).then_inc(qs_ready.sem, 1)
                dve.wait_ge(qs_ready.sem, qs_ready.at(b, 1))
                nc.vector.tensor_tensor(qs[:, :, 32:64], x1_v, qs[:, :, 0:32], ALU.subtract).then_inc(qs_ready.sem, 1)

            def a_pack(b, p):
                dve.wait_ge(qp_mm.sem, qp_mm.at(b))
                dve.wait_ge(s_mm.sem, s_mm.back(b, 2))
                src = pa[0][:, 0:PAIRS * T // 2].bitcast(F16).rearrange("p (g t) -> p g t", g=PAIRS)
                for h in range(2):
                    nc.vector.tensor_scalar(qp[:, p, :, h], src, pick[:, h:h + 1], None, ALU.mult).then_inc(qp_ready.sem, 1)

            def b_max(half):
                def step(b, p):
                    for h in range(8 * half, 8 * half + 8):
                        dve.wait_ge(max_mm.sem, max_mm.at(b, h + 1))
                        if h == 0:
                            dve.wait_ge(nm_ready.sem, nm_ready.back(b))
                        nc.vector.tensor_reduce(mx[:, h:h + 1], psc[h % 2][0:T, 0:S2], AX_X, ALU.max).then_inc(max_ready.sem, 1)
                return step

            def b_shift(b, p):
                dve.wait_ge(max_ready.sem, max_ready.at(b))
                dve.wait_ge(nmt_mm.sem, nmt_mm.back(b))
                nc.vector.tensor_scalar(nm[:], mx[:], -1.0 / SHIFT, None, ALU.mult).then_inc(nm_ready.sem, 1)

            def b_normalize(b, p):
                dve.wait_ge(bot_mm.sem, bot_mm.at(b))
                sums = psc[0][0:T, 0:512].rearrange("p (h r) -> p h r", h=H)
                nc.vector.reciprocal(rdb[:].unsqueeze(2), sums[:, :, DH:V1]).then_inc(rdb_ready.sem, 1)
                dve.wait_ge(rdb_ready.sem, rdb_ready.at(b))
                dve.wait_ge(bnt_mm.sem, bnt_mm.back(b))
                nc.vector.tensor_tensor(bn[:].rearrange("p (h d) -> p h d", h=H), sums[:, :, 0:DH],
                                        rdb[:].unsqueeze(2).to_broadcast([T, H, DH]), ALU.mult).then_inc(bn_ready.sem, 1)

            def b_output(b, p):
                dve.wait_ge(fc_mm.sem, fc_mm.at(b))
                dve.wait_ge(x1b_ready.sem, x1b_ready.at(b))
                nc.vector.tensor_tensor(rb[:], psc[0][0:T, 0:D], x1b[:], ALU.add).then_inc(rb_ready.sem, 1)
                dve.wait_ge(rb_ready.sem, rb_ready.at(b))
                normalized(b, rb[:], stb, mvb, rsb, stb_ready, mvb_ready, rsb_ready, x2[:, p], x2_ready)

            def b_route(b, p):
                dve.wait_ge(lg_mm.sem, lg_mm.at(b))
                nc.vector.tensor_copy(lg[:], psc[0][0:T, 0:E]).then_inc(lg_ready.sem, 1)
                hold(dve, lg_ready.sem, lg_ready.at(b))
                nc.vector.max(m8[:], lg[:]).then_inc(route.sem, 1)
                dve.wait_ge(route.sem, route.at(b, 1))
                nc.vector.tensor_scalar(nm0[:], m8[:, 0:1], -1.0, None, ALU.mult).then_inc(route.sem, 1)
                nc.vector.max_index(i8[:], m8[:], lg[:]).then_inc(route.sem, 1)
                dve.wait_ge(route.sem, route.at(b, 3))
                nc.vector.tensor_copy(i8f[:], i8[:, 0:2]).then_inc(route.sem, 1)
                dve.wait_ge(ee_ready.sem, ee_ready.at(b))
                nc.vector.tensor_tensor(es[:], ee[:, 0:1], ee[:, 1:2], ALU.add).then_inc(route.sem, 1)
                dve.wait_ge(route.sem, route.at(b, 5))
                nc.vector.reciprocal(er[:], es[:]).then_inc(route.sem, 1)
                dve.wait_ge(route.sem, route.at(b, 6))
                nc.vector.tensor_scalar(gg[:], ee[:], er[:, 0:1], 0.5, ALU.mult, ALU.mult).then_inc(route.sem, 1)
                dve.wait_ge(route.sem, route.at(b, 7))
                for n in range(2):
                    last = nc.vector.tensor_scalar(g01[:, n], pick[0:T, 2:2 + E], i8f[:, n:n + 1], gg[:, n:n + 1],
                                                   ALU.is_equal, ALU.mult)
                last.then_inc(route.sem, 1)
                dve.wait_ge(route.sem, route.at(b, 8))
                nc.vector.tensor_tensor(gate[:, p], g01[:, 0], g01[:, 1], ALU.add).then_inc(gate_ready.sem, 1)

            def gated(b, p, e):
                dve.wait_ge(dn_mm.sem, dn_mm.at(b, e + 1))
                if e == 0:
                    dve.wait_ge(gate_ready.sem, gate_ready.at(b))
                    dve.wait_ge(y_ready.sem, y_ready.back(b))
                    prev = x2[:, p]
                else:
                    dve.wait_ge(acc_ready.sem, acc_ready.at(b, e))
                    prev = acc[:, (e - 1) % 2]
                nc.vector.scalar_tensor_tensor(out=acc[:, e % 2], in0=pd[0:T, 0:D], scalar=gate[:, p, e:e + 1], in1=prev,
                                               op0=ALU.mult, op1=ALU.add).then_inc(acc_ready.sem, 1)

            def c_expert(e):
                def step(b, p):
                    dve.wait_ge(th_ready.sem, th_ready.at(b, e + 1))
                    dve.wait_ge(up_mm.sem, up_mm.at(b, e + 1))
                    if e >= 2:
                        dve.wait_ge(hd_ready.sem, hd_ready.at(b, e - 1))
                    else:
                        dve.wait_ge(hd_ready.sem, hd_ready.back(b))
                    nc.vector.scalar_tensor_tensor(out=w1[:, e % 2], in0=th[:, e % 2], scalar=1.0, in1=pu[e % 2][:, 0:2 * T],
                                                   op0=ALU.add, op1=ALU.mult).then_inc(w1_ready.sem, 1)
                    dve.wait_ge(w1_ready.sem, w1_ready.at(b, e + 1))
                    if e >= 2:
                        dve.wait_ge(dn_mm.sem, dn_mm.at(b, e - 1))
                    else:
                        dve.wait_ge(dn_mm.sem, dn_mm.back(b))
                    nc.vector.tensor_tensor(hd[:, e % 2], w1[:, e % 2], pu[e % 2][:, 2 * T:4 * T], ALU.mult).then_inc(hd_ready.sem, 1)
                    if e >= 1:
                        gated(b, p, e - 1)
                return step

            def c_finish(b, p):
                gated(b, p, E - 1)
                dve.wait_ge(acc_ready.sem, acc_ready.at(b))
                dve.wait_ge(y_out.sem[p], y_out.back(b, p))
                normalized(b, acc[:, (E - 1) % 2], stc, mvc, rsc, stc_ready, mvc_ready, rsc_ready, yo[:, p], y_ready)

            dve.wait_ge(mask_in, 16)
            nc.vector.tensor_scalar(mask_h[:], mask_i[:], 0.0, -BIG, ALU.is_equal, ALU.mult).then_inc(mask_ready, 1)
            nc.vector.memset(ppv[:], 0.0).then_inc(vector_presets, 1)
            nc.vector.memset(v1[:, :, DH:V1], 1.0).then_inc(vector_presets, 1)
            dve.wait_ge(weights_in, WEIGHTS)
            nc.vector.tensor_copy(idh[:], idn[:]).then_inc(ident_ready, 1)
            dve.wait_ge(presets, PRESETS)
            pipeline(dve, {
                ("A", "project"): a_project, ("A", "normalize"): a_normalize, ("A", "output"): a_output, ("A", "pack"): a_pack,
                ("B", "max0"): b_max(0), ("B", "max1"): b_max(1), ("B", "shift"): b_shift, ("B", "normalize"): b_normalize,
                ("B", "output"): b_output, ("B", "route"): b_route, ("C", "finish"): c_finish,
            } | {("C", f"expert{e}"): c_expert(e) for e in range(E)})

        @block.gpsimd
        def _(pool):
            def after(n, value):
                if not isinstance(value, int) or value > 0:
                    hold(pool, n.sem, value)

            def keys(b, p, part):
                if part == 0:
                    after(xbo_ready, xbo_ready.at(b))
                    hold(pool, ctx_in.sem[p], ctx_in.at(b, p))
                    hold(pool, s_mm.sem, s_mm.back(b, 2))
                    nc.gpsimd.tensor_copy(kp[0:96, p], kc[:, p]).then_inc(kp_ready.sem, 1)
                else:
                    after(x1b_ready, x1b_ready.back(b))
                    pool.wait_ge(kp_ready.sem, kp_ready.at(b, 1))
                    nc.gpsimd.tensor_tensor(kp[64:96, p], kc[64:96, p], kp[64:96, p], ALU.subtract).then_inc(kp_ready.sem, 1)

            def inverse_root(b, mv, mean_var, rs, rsr):
                hold(pool, mv.sem, mv.at(b))
                nc.gpsimd.tensor_scalar(rs[:, 0:1], mean_var[:, 1:2], LN_EPS, None, ALU.add).then_inc(rsr.sem, 1)
                pool.wait_ge(rsr.sem, rsr.at(b, 1))
                nc.gpsimd.tensor_tensor(rs[:, 1:2], rs[:, 0:1], pick[0:T, 2 + E:3 + E], ALU.pow).then_inc(rsr.sem, 1)

            def a_project(b, p):
                after(rsc_ready, rsc_ready.back(b, 3))
                for n, ready in ((0, q_ready), (1, k_ready)):
                    pool.wait_ge(ready.sem, ready.at(b))
                    if n == 1:
                        after(squares, squares.at(b, 1))
                    nc.gpsimd.tensor_tensor(qk[64:128, n], qk[64:128, n], qk[64:128, n], ALU.mult).then_inc(squares.sem, 1)

            def a_features(b, p):
                for i in range(2):
                    if i == 0:
                        after(squares, squares.at(b))
                    else:
                        after(kf_ready, kf_ready.at(b, 1))
                    hold(pool, kf_exp.sem, kf_exp.at(b, i + 1))
                    nc.gpsimd.tensor_scalar(kf[:, i * 512:i * 512 + 512], kf[:, i * 512:i * 512 + 512], FEATURE_EPS, None,
                                            ALU.add).then_inc(kf_ready.sem, 1)
                for u in range(2):
                    if u == 0:
                        after(kf_ready, kf_ready.at(b))
                    else:
                        after(qf_ready, qf_ready.at(b, 1))
                    hold(pool, qf_exp.sem, qf_exp.at(b, u + 1))
                    nc.gpsimd.tensor_scalar(qf[:, u], qf[:, u], FEATURE_EPS, None, ALU.add).then_inc(qf_ready.sem, 1)
                after(qf_ready, qf_ready.at(b))
                pool.wait_ge(x_in.sem[p], x_in.at(b, p))
                pool.wait_ge(ra_ready.sem, ra_ready.back(b))
                nc.gpsimd.tensor_tensor(xbo[:], xr[:, p], bo[:], ALU.add).then_inc(xbo_ready.sem, 1)

            def a_kv(b, p):
                keys(b, p, 0)

            def a_read(b, p):
                keys(b, p, 1)

            def a_output(b, p):
                after(kp_ready, kp_ready.at(b))
                inverse_root(b, mva_ready, mva, rsa, rsa_ready)

            def b_shift(b, p):
                if isinstance(b, int) and b == B - 1:
                    after(rsa_ready, rsa_ready.at(b))
                else:
                    after(kp_ready, kp_ready.at(b + 1, 1))
                pool.wait_ge(x1_ready.sem, x1_ready.at(b))
                pool.wait_ge(rb_ready.sem, rb_ready.back(b))
                nc.gpsimd.tensor_tensor(x1b[:], x1[:, p], bfc[:], ALU.add).then_inc(x1b_ready.sem, 1)

            def b_output(b, p):
                if isinstance(b, int) and b == B - 1:
                    after(x1b_ready, x1b_ready.at(b))
                else:
                    after(rsa_ready, rsa_ready.at(b + 1))
                inverse_root(b, mvb_ready, mvb, rsb, rsb_ready)

            def c_finish(b, p):
                if not (isinstance(b, int) and b == B - 1):
                    after(rsb_ready, rsb_ready.at(b + 1))
                inverse_root(b, mvc_ready, mvc, rsc, rsc_ready)

            nc.gpsimd.memset(bd[:], 0.0).then_inc(presets, 1)
            pool.wait_ge(presets, 1)
            nc.gpsimd.memset(qs[:, :, 96:128], 0.0).then_inc(presets, 1)
            pool.wait_ge(presets, 2)
            nc.gpsimd.memset(kp[96:128], 0.0).then_inc(presets, 1)
            pool.wait_ge(presets, 3)
            nc.gpsimd.memset(qs[:, :, 97:98], BIG).then_inc(presets, 1)
            pool.wait_ge(presets, 4)
            nc.gpsimd.memset(kp[96:97], SHIFT).then_inc(presets, 1)
            pool.wait_ge(presets, 5)
            pool.wait_ge(weights_in, WEIGHTS)
            pipeline(pool, {
                ("A", "project"): a_project, ("A", "features"): a_features, ("A", "kv"): a_kv, ("A", "read"): a_read,
                ("A", "output"): a_output, ("B", "shift"): b_shift, ("B", "output"): b_output, ("C", "finish"): c_finish,
            })


def kernel(**inputs):
    import numpy as np
    import concourse.bacc as bacc
    from concourse.bass_utils import run_bass_kernel_spmd

    f = {n: np.asarray(a) for n, a in inputs.items()}
    x, c = f["x"], f["ctx_1024"]

    def rows128(w):
        return w.reshape(-1, 128, w.shape[-1]).transpose(1, 0, 2)

    def doubled(w):
        t = rows128(w.T).reshape(128, KT, 4, 1, 64)
        return np.broadcast_to(t, (128, KT, 4, 2, 64)).reshape(128, KT, 4, 128)

    def doubled_bias(v):
        return np.broadcast_to(v.reshape(4, 1, 64), (4, 2, 64)).reshape(4, 128).T

    def every_token(v):
        return np.broadcast_to(v, (T, D))

    orf_rows = np.zeros((128, 4, M), np.float32)
    for h in range(4):
        orf_rows[h * DH:(h + 1) * DH, h] = f["L0_attn_orf"].T
        orf_rows[64 + h * DH:64 + (h + 1) * DH, h] = -0.25
    picks = np.zeros((128, 2 + E + 1), np.float32)
    for p in range(128):
        picks[p, 0] = p >= 96 or p % 32 < DH
        picks[p, 1] = p >= 96 or p % 32 >= DH
    picks[:, 2:2 + E] = np.arange(E)
    picks[:, 2 + E] = -0.5
    values = np.ones((B, CH, NC, H, V1), np.float32)
    values[..., :DH] = c.reshape(B, NC, CH, H, DH).transpose(0, 2, 1, 3, 4)

    arrays = {
        "x_rows": x,
        "x_cols": x.transpose(0, 2, 1).reshape(B, KT, 128, T).transpose(0, 2, 1, 3),
        "ctx_cols": c.transpose(0, 2, 1).reshape(B, PAIRS, 32, S2).transpose(0, 2, 1, 3),
        "ctx_rows": values,
        "mask": f["mask_Bx1x1xS2_ik0"].reshape(1, B * S2).astype(np.int32),
        "w_q": doubled(f["L0_attn_Wq"]), "w_k": doubled(f["L0_attn_Wk"]),
        "w_v": rows128(f["L0_attn_Wv"].T), "w_o": rows128(f["L0_attn_Wo"].T), "w_fc": rows128(f["L0_xattn_fc_w"].T),
        "b_qk": np.stack([doubled_bias(f["L0_attn_bq"]), doubled_bias(f["L0_attn_bk"])], 1),
        "b_v": every_token(f["L0_attn_bv"]), "b_o": every_token(f["L0_attn_bo"]), "b_fc": every_token(f["L0_xattn_fc_b"]),
        "orf_rows": orf_rows.reshape(128, 4 * M),
        "w_router": rows128(f["L0_ffn_router_w"].T),
        "w_up": f["L0_ffn_up_proj"].reshape(E, KT, 128, 2 * DE).transpose(2, 0, 1, 3),
        "w_down": f["L0_ffn_down_proj"].reshape(E, DE // 128, 128, D).transpose(2, 0, 1, 3),
        "ident": np.eye(128, dtype=np.float32),
        "picks": picks,
    }
    nc = bacc.Bacc("TRN2", target_bir_lowering=False, num_devices=1)
    feeds, args = {}, {}
    for name, a in arrays.items():
        a = np.ascontiguousarray(a)
        feeds[f"in_{name}"] = a
        args[name] = nc.dram_tensor(f"in_{name}", a.shape, mybir.dt.from_np(a.dtype), kind="ExternalInput").ap()
    args["out"] = nc.dram_tensor("out", (B, T, D), F32, kind="ExternalOutput").ap()
    build(nc, **args)
    r = run_bass_kernel_spmd(nc, [feeds], core_ids=[0])
    return r.results[0]["out"]
```

```python
from contextlib import ExitStack

import concourse.bass as bass
from concourse import mybir

F32 = mybir.dt.float32
F16 = mybir.dt.float16
I32 = mybir.dt.int32
U32 = mybir.dt.uint32
ACT = mybir.ActivationFunctionType
ALU = mybir.AluOpType
AX_X = mybir.AxisListType.X

B, T, D = 8, 112, 256
S2, CH = 375, 125
NC = S2 // CH
H, DH, M = 16, 16, 64
KT = D // 128
E, DE = 8, 256
PAIRS = H // 2
QUADS = H // 4
V1 = DH + 1
FEATURE_EPS = 1e-6
LN_EPS = 1e-5
SHIFT = 64.0
BIG = 60000.0

WSCALE = 64.0

EXPERTS = (["up_a0", "up_b0", "up_a1", "up_b1", "down0"]
           + [f"{s}{e - (s == 'down')}" for e in range(2, E) for s in ("up_a", "up_b", "down")]
           + ["gap", f"down{E - 1}", "finish", "store"])
MAIN = """
    A.qk B.max0 C A.v B.max1 C B.max2 C A.high0 B.max3 C A.k_features B.max4 C A.q_features B.max5 C
    A.high1 B.max6 C A.kv B.max7 C B.shift A.read C B.unit0 B.unit1 C A.normalize B.unit2 C A.low0 B.unit3 C
    A.turn B.unit4 A.low1 B.unit5 C B.unit6 C A.output B.unit7 C A.low2 B.unit8 C A.apply B.unit9 C A.low3 B.unit10 C
    B.unit11 A.pack C B.gather C B.normalize C B.turn C B.output C B.apply C B.turn_x C B.logits C C
"""


def order():
    experts = iter(EXPERTS)
    steps = [("C", next(experts)) if s == "C" else tuple(s.split(".")) for s in MAIN.split()]
    assert next(experts, None) is None
    return steps


ORDER = order()
LAG = {"A": 0, "B": 1, "C": 2}


class Count:

    def __init__(self, nc, ctx, name, per=1):
        self.sem = ctx.enter_context(nc.semaphore(name))
        self.per = per
        nc.sync.sem_inc(self.sem, 2 * self.per)

    def at(self, b, k=None):
        return b * self.per + (2 * self.per + (self.per if k is None else k))

    def back(self, b, depth=1):
        return b * self.per + (3 - depth) * self.per


class Landing:

    def __init__(self, nc, ctx, name, n=1):
        self.rise = 16 * n
        self.sem = [ctx.enter_context(nc.semaphore(f"{name}{p}")) for p in range(2)]
        for s in self.sem:
            nc.sync.sem_inc(s, self.rise)

    def at(self, b, p):
        return (b - p) * (self.rise // 2) + 2 * self.rise

    def back(self, b, p):
        return (b - p) * (self.rise // 2) + self.rise


def build(nc, x_rows, x_cols, ctx_cols, ctx_rows, mask, w_q, w_k, w_v, w_o, w_fc, b_qk, b_v, b_o, b_fc,
          orf_rows, w_router, w_experts, ident, picks, out):
    with ExitStack() as ctx:
        def sb(name, shape, dt=F32):
            return ctx.enter_context(nc.sbuf_tensor(name, shape, dt))

        def bank(name):
            return ctx.enter_context(nc.psum_tensor(name, [128, 512], F32))

        def sem(name):
            return ctx.enter_context(nc.semaphore(name))

        wqk = sb("wqk", [128, 2, KT, D])
        wv = sb("wv", [128, KT, D])
        wo = sb("wo", [128, KT, D])
        wfc = sb("wfc", [128, KT, D])
        wr = sb("wr", [128, KT, E])
        wr_h, wr_l = sb("wr_h", [128, KT, E], F16), sb("wr_l", [128, KT, E], F16)
        EW = KT * 2 * DE + DE // 128 * D
        NX = 3
        wex = sb("wex", [128, NX, EW])
        wex_h, wex_l = sb("wex_h", [128, E, EW], F16), sb("wex_l", [128, E, EW], F16)
        bqk = sb("bqk", [128, 2, KT])
        bv = sb("bv", [T, D])
        bo = sb("bo", [128, D])
        bfc = sb("bfc", [128, D])
        orf = sb("orf", [128, 4 * M])
        idn = sb("idn", [128, 128])
        idh = sb("idh", [128, 128], F16)
        pick = sb("pick", [128, 2 + E + 1])
        mask_i = sb("mask_i", [1, B * S2], I32)
        mask_h = sb("mask_h", [1, B * S2], F16)

        xr = sb("xr", [128, 2, D])
        xc = sb("xc", [128, 2, KT, T])
        xbo = sb("xbo", [128, D])
        qk = sb("qk", [128, 2, 4, T])
        v1 = sb("v1", [T, H, V1])
        kf = sb("kf", [128, H * M])
        qf = sb("qf", [128, 2, 4, T])
        bd = sb("bd", [128, PAIRS, 64])
        ao = sb("ao", [128, 4, T])
        rda = sb("rda", [T, H])
        an = sb("an", [T, D])
        ant = sb("ant", [128, KT, T])
        ra = sb("ra", [T, D])
        sta = sb("sta", [T, 6])
        mva = sb("mva", [128, 2])
        rsa = sb("rsa", [128, 2])
        x1 = sb("x1", [128, 2, D])
        qs = sb("qs", [T, PAIRS, 128], F16)
        qp = sb("qp", [128, 2, PAIRS, 2, T], F16)

        kc = sb("kc", [96, 2, PAIRS, S2])
        kp = sb("kp", [128, 2, PAIRS, S2], F16)
        vx = sb("vx", [CH, 2, NC, H, V1])
        x1b = sb("x1b", [128, D])
        mx = sb("mx", [T, H])
        nm = sb("nm", [T, H], F16)
        NP = 4
        pr = sb("pr", [CH, NP, 4 * T])
        bo2 = sb("bo2", [128, QUADS, T])
        rdb = sb("rdb", [T, H])
        bn = sb("bn", [T, D])
        bnt = sb("bnt", [128, KT, T])
        rb = sb("rb", [T, D])
        stb = sb("stb", [T, 6])
        mvb = sb("mvb", [128, 2])
        rsb = sb("rsb", [128, 2])
        x2 = sb("x2", [T, 2, D])
        x2h, x2l = sb("x2h", [128, 2, KT, T], F16), sb("x2l", [128, 2, KT, T], F16)
        lg = sb("lg", [T, E])
        m8 = sb("m8", [T, 8])
        i8 = sb("i8", [T, 8], U32)
        i8f = sb("i8f", [T, 2])
        nm0 = sb("nm0", [T, 1])
        ee = sb("ee", [T, 2])
        es = sb("es", [T, 1])
        er = sb("er", [T, 1])
        gg = sb("gg", [T, 2])
        g01 = sb("g01", [T, 2, E])
        gate = sb("gate", [T, 2, E])

        th = sb("th", [128, 2, 2 * T])
        w1 = sb("w1", [128, 2, 2 * T])
        hd = sb("hd", [128, 2, 2 * T])
        hd_h, hd_l = sb("hd_h", [128, 2, 2 * T], F16), sb("hd_l", [128, 2, 2 * T], F16)
        acc = sb("acc", [T, 2, D])
        stc = sb("stc", [T, 6])
        mvc = sb("mvc", [128, 2])
        rsc = sb("rsc", [128, 2])
        yo = sb("yo", [T, 2, D])

        pa = [bank("pa0"), bank("pa1")]
        psc = [bank("ps0"), bank("ps1")]
        ppv = bank("ppv")
        pu = [bank("pu0"), bank("pu1")]
        pd = bank("pd")

        qk_weights_in, v_weights_in, consts_in = sem("qk_weights_in"), sem("v_weights_in"), sem("consts_in")
        tail_weights_in = sem("tail_weights_in")
        experts_in = [sem(f"experts_in{e}") for e in range(E)]
        high_weights, low_weights = sem("high_weights"), sem("low_weights")
        mask_in = sem("mask_in")
        mask_ready = sem("mask_ready")
        ident_ready = sem("ident_ready")
        vector_presets = sem("vector_presets")
        presets = sem("presets")

        def count(name, per=1):
            return Count(nc, ctx, name, per)

        x_in, ctx_in = Landing(nc, ctx, "x_in", 2), Landing(nc, ctx, "ctx_in", 3)
        v_in, mrow_in = Landing(nc, ctx, "v_in"), Landing(nc, ctx, "mrow_in")
        y_out = Landing(nc, ctx, "y_out")
        qk_mm, v_mm = count("qk_mm"), count("v_mm")
        qk_ready, v_ready = count("qk_ready", 2), count("v_ready")
        squares = count("squares")
        kf_mm, qf_mm = count("kf_mm", 2), count("qf_mm", 2)
        kf_exp, qf_exp = count("kf_exp", 2), count("qf_exp", 2)
        kf_ready, qf_ready = count("kf_ready", 2), count("qf_ready", 2)
        kv_mm, bd_ready = count("kv_mm"), count("bd_ready", 2)
        ao_mm, ao_ready = count("ao_mm"), count("ao_ready")
        aot_mm, rda_ready, an_ready = count("aot_mm"), count("rda_ready"), count("an_ready")
        ant_mm, ant_ready = count("ant_mm"), count("ant_ready")
        wo_mm, xbo_ready, ra_ready = count("wo_mm"), count("xbo_ready"), count("ra_ready")
        sta_ready, mva_ready, rsa_ready = count("sta_ready"), count("mva_ready"), count("rsa_ready", 2)
        x1_ready, qs_ready = count("x1_ready"), count("qs_ready", 2)
        qp_mm, qp_ready = count("qp_mm"), count("qp_ready", 2)
        kp_high, kp_low = count("kp_high", 2), count("kp_low", 4)
        max_mm, max_ready = count("max_mm", H), count("max_ready", H)
        nm_ready, nmt_mm, nmrow_ready = count("nm_ready"), count("nmt_mm", 2), count("nmrow_ready", 2)
        s_mm, p_ready, pv_mm = count("s_mm", QUADS * NC), count("p_ready", QUADS * NC), count("pv_mm", QUADS * NC)
        bo2_ready, bot_mm = count("bo2_ready"), count("bot_mm")
        rdb_ready, bn_ready = count("rdb_ready"), count("bn_ready")
        bnt_mm, bnt_ready, fc_mm = count("bnt_mm"), count("bnt_ready"), count("fc_mm")
        x1b_ready, rb_ready, stb_ready = count("x1b_ready"), count("rb_ready"), count("stb_ready")
        mvb_ready, rsb_ready, x2_ready = count("mvb_ready"), count("rsb_ready", 2), count("x2_ready")
        x2t_mm, x2h_ready, x2l_ready, lg_mm, lg_ready = count("x2t_mm"), count("x2h_ready"), count("x2l_ready"), count("lg_mm"), count("lg_ready")
        route = count("route", 8)
        ee_ready, gate_ready = count("ee_ready"), count("gate_ready")
        hd_high, hd_low = count("hd_high", E), count("hd_low", E)
        up_mm, th_ready, w1_ready, hd_ready = (count(n, E) for n in ("up_mm", "th_ready", "w1_ready", "hd_ready"))
        dn_mm, acc_ready = count("dn_mm", E), count("acc_ready", E)
        stc_ready, mvc_ready, rsc_ready = count("stc_ready"), count("mvc_ready"), count("rsc_ready", 2)
        y_ready = count("y_ready")

        waited = sem("waited")

        def hold(eng, sem_, value):
            eng.wait_ge(sem_, value)
            eng.sem_inc(waited, 1)

        PRESETS = 13

        block = ctx.enter_context(nc.Block())

        def iteration(steps, i, half, stages):
            for stage, step in ORDER:
                if stage == "C" and "W" in stages:
                    n = EXPERTS.index(step)
                    if ("W", "split") in steps and n % 6 == 1 and n // 6 < E // 2:
                        steps["W", "split"](i * (E // 2) + n // 6)
                elif stage in stages and (stage, step) in steps:
                    steps[stage, step](i - LAG[stage], (half - LAG[stage]) % 2)

        def pipeline(eng, steps):
            iteration(steps, 0, 0, "AW")
            iteration(steps, 1, 1, "ABW")
            with eng.Fori(2, B - 1, 2) as i:
                iteration(steps, i, 0, "ABC")
                iteration(steps, i + 1, 1, "ABC")
            iteration(steps, B, B % 2, "BC")
            iteration(steps, B + 1, (B + 1) % 2, "C")

        @block.sync
        def _(sp):
            def load_x(b, p):
                sp.wait_ge(xbo_ready.sem, xbo_ready.back(b, 2))
                sp.wait_ge(v_mm.sem, v_mm.back(b, 2))
                sp.dma_start(xc[:, p], x_cols[bass.ds(b, 1)].rearrange("o p k t -> (o p) k t")).then_inc(x_in.sem[p], 16)
                sp.dma_start(xr[0:T, p, :], x_rows[bass.ds(b, 1)].rearrange("o t d -> (o t) d")).then_inc(x_in.sem[p], 16)

            def load_context(b, p):
                sp.wait_ge(kp_low.sem, kp_low.back(b, 2))
                for r in range(3):
                    sp.dma_start(kc[32 * r:32 * r + 32, p], ctx_cols[bass.ds(b, 1)].rearrange("o r g s -> (o r) g s")).then_inc(ctx_in.sem[p], 16)
                sp.wait_ge(pv_mm.sem, pv_mm.back(b, 2))
                sp.dma_start(vx[:, p], ctx_rows[bass.ds(b, 1)].rearrange("o s c h v -> (o s) c h v")).then_inc(v_in.sem[p], 16)
                sp.wait_ge(s_mm.sem, s_mm.back(b, 2))
                sp.dma_start(kp[97:98, p], mask_h[0:1, bass.ds(b * S2, S2)].rearrange("o (u s) -> o u s", u=1).to_broadcast([1, PAIRS, S2])).then_inc(mrow_in.sem[p], 16)

            for dst, src, done in (
                    (wqk[:, 0], w_q, qk_weights_in), (wqk[:, 1], w_k, qk_weights_in), (bqk[:], b_qk, qk_weights_in),
                    (orf[:], orf_rows, qk_weights_in), (wv[:], w_v, v_weights_in), (bv[:], b_v, v_weights_in),
                    (idn[:], ident, consts_in), (pick[:], picks, consts_in), (mask_i[:], mask, mask_in)):
                if src is w_v:
                    sp.wait_ge(presets, 1)
                    load_x(0, 0)
                sp.dma_start(dst, src).then_inc(done, 16)
            sp.wait_ge(mask_ready, 1)
            sp.wait_ge(presets, PRESETS)
            load_context(0, 0)
            for dst, src in ((bo[0:T], b_o), (wo[:], w_o), (wr[:], w_router), (wfc[:], w_fc), (bfc[0:T], b_fc)):
                sp.dma_start(dst, src).then_inc(tail_weights_in, 16)
            for e in range(2):
                sp.dma_start(wex[:, e % NX], w_experts[:, e]).then_inc(experts_in[e], 16)
            load_x(1, 1)
            load_context(1, 1)
            for e in range(2, E):
                if e >= NX:
                    sp.wait_ge(low_weights, 1 + e - NX + 1)
                sp.dma_start(wex[:, e % NX], w_experts[:, e]).then_inc(experts_in[e], 16)
            with sp.Fori(2, B - 1, 2) as b:
                load_x(b, 0)
                load_context(b, 0)
                load_x(b + 1, 1)
                load_context(b + 1, 1)
            for b in (B - 2, B - 1):
                sp.wait_ge(y_out.sem[b % 2], y_out.at(b, b % 2))

        @block.tensor
        def _(pe):
            def a_qk(b, p):
                if isinstance(b, int) and b == 0:
                    pe.wait_ge(qk_weights_in, 4 * 16)
                pe.wait_ge(x_in.sem[p], x_in.at(b, p))
                pe.wait_ge(ra_ready.sem, ra_ready.back(b))
                for n in range(2):
                    for c in range(KT):
                        for k in range(KT):
                            mm = nc.tensor.matmul(pa[0][:, (n * KT + c) * T:(n * KT + c + 1) * T],
                                                  wqk[:, n, k, c * 128:c * 128 + 128], xc[:, p, k],
                                                  start=(k == 0), stop=(k == KT - 1))
                mm.then_inc(qk_mm.sem, 1)

            def a_v(b, p):
                if isinstance(b, int) and b == 0:
                    pe.wait_ge(v_weights_in, 2 * 16)
                pe.wait_ge(qp_ready.sem, qp_ready.back(b))
                for k in range(KT):
                    mm = nc.tensor.matmul(pa[1][0:T, 0:D], xc[:, p, k], wv[:, k], start=(k == 0), stop=(k == KT - 1))
                mm.then_inc(v_mm.sem, 1)

            def a_k_features(b, p):
                pe.wait_ge(squares.sem, squares.at(b))
                for i in range(2):
                    if i == 1:
                        pe.wait_ge(v_ready.sem, v_ready.at(b))
                    for t in (2 * i, 2 * i + 1):
                        mm = nc.tensor.matmul(pa[i][0:T, (t % 2) * 256:(t % 2) * 256 + 256], qk[:, 1, t], orf[:],
                                              start=True, stop=True)
                    mm.then_inc(kf_mm.sem, 1)

            def a_q_features(b, p):
                for u in range(2):
                    pe.wait_ge(kf_exp.sem, kf_exp.at(b, u + 1))
                    mm = nc.tensor.matmul(pa[u][:, 0:4 * T], orf[:, u * 128:u * 128 + 128],
                                          qk[:, 0].rearrange("p t n -> p (t n)"), start=True, stop=True)
                    mm.then_inc(qf_mm.sem, 1)

            def a_kv(b, p):
                pe.wait_ge(kf_ready.sem, kf_ready.at(b))
                pe.wait_ge(qf_exp.sem, qf_exp.at(b, 1))
                for h in range(H):
                    r, c = 64 * (h % 2), h * V1
                    mm = nc.tensor.matmul(pa[0][r:r + 64, c:c + V1], kf[0:T, h * M:(h + 1) * M], v1[:, h],
                                          start=True, stop=True)
                mm.then_inc(kv_mm.sem, 1)

            def a_read(b, p):
                pe.wait_ge(bd_ready.sem, bd_ready.at(b))
                pe.wait_ge(qf_ready.sem, qf_ready.at(b))
                for j in range(PAIRS):
                    r, c = 64 * (j % 2), j // 2
                    mm = nc.tensor.matmul(pa[1][r:r + 64, c * T:(c + 1) * T], bd[:, j], qf[:, j % 2, j // 2],
                                          start=True, stop=True)
                mm.then_inc(ao_mm.sem, 1)

            def a_normalize(b, p):
                if isinstance(b, int) and b == 0:
                    pe.wait_ge(consts_in, 2 * 16)
                pe.wait_ge(ao_ready.sem, ao_ready.at(b))
                for c in range(4):
                    mm = nc.tensor.transpose(pa[0][0:T, c * 128:c * 128 + 128], ao[:, c], idn[:])
                mm.then_inc(aot_mm.sem, 1)

            def a_turn(b, p):
                pe.wait_ge(an_ready.sem, an_ready.at(b))
                for k in range(KT):
                    mm = nc.tensor.transpose(pa[1][:, k * T:(k + 1) * T], an[:, k * 128:k * 128 + 128], idn[0:T, 0:T])
                mm.then_inc(ant_mm.sem, 1)

            def a_output(b, p):
                if isinstance(b, int) and b == 0:
                    pe.wait_ge(tail_weights_in, 5 * 16)
                pe.wait_ge(ant_ready.sem, ant_ready.at(b))
                for k in range(KT):
                    mm = nc.tensor.matmul(pa[0][0:T, 0:D], ant[:, k], wo[:, k], start=(k == 0), stop=(k == KT - 1))
                mm.then_inc(wo_mm.sem, 1)

            def a_pack(b, p):
                pe.wait_ge(qs_ready.sem, qs_ready.at(b))
                if isinstance(b, int) and b == 0:
                    pe.wait_ge(ident_ready, 1)
                dst = pa[1][:, 0:PAIRS * T // 2].bitcast(F16)
                for g in range(PAIRS):
                    mm = nc.tensor.transpose(dst[:, g * T:(g + 1) * T], qs[:, g], idh[0:T, 0:T])
                mm.then_inc(qp_mm.sem, 1)

            def b_max(n):
                def step(b, p):
                    if n == 0:
                        pe.wait_ge(qp_ready.sem, qp_ready.at(b))
                        pe.wait_ge(kp_low.sem, kp_low.at(b))
                        pe.wait_ge(mrow_in.sem[p], mrow_in.at(b, p))
                        pe.wait_ge(lg_ready.sem, lg_ready.back(b))
                    for h in (2 * n, 2 * n + 1):
                        if h == 1:
                            pe.wait_ge(x2l_ready.sem, x2l_ready.back(b))
                        elif h >= 2:
                            pe.wait_ge(max_ready.sem, max_ready.at(b, h - 1))
                        nc.tensor.matmul(psc[h % 2][0:T, 0:S2], qp[:, p, h // 2, h % 2], kp[:, p, h // 2],
                                         start=True, stop=True).then_inc(max_mm.sem, 1)
                return step

            def b_shift(b, p):
                pe.wait_ge(nm_ready.sem, nm_ready.at(b))
                for n in range(2):
                    dst = psc[n][:, 0:8 * T // 2].bitcast(F16)
                    for h in range(8):
                        mm = nc.tensor.transpose(dst[96:97, h * T:(h + 1) * T], nm[:, 8 * n + h:8 * n + h + 1],
                                                 idh[0:T, 0:T], tile_position=(0, 96))
                    mm.then_inc(nmt_mm.sem, 1)

            def values(b, p, u):
                q, c = u // NC, u % NC
                pe.wait_ge(p_ready.sem, p_ready.at(b, u + 1))
                if u == 0:
                    pe.wait_ge(v_in.sem[p], v_in.at(b, p))
                    pe.wait_ge(bo2_ready.sem, bo2_ready.back(b))
                for j in range(4):
                    mm = nc.tensor.matmul(ppv[32 * j:32 * j + V1, q * T:(q + 1) * T], vx[:, p, c, 4 * q + j],
                                          pr[:, u % NP, j * T:(j + 1) * T], start=(c == 0), stop=(c == NC - 1))
                mm.then_inc(pv_mm.sem, 1)

            def b_unit(u):
                def step(b, p):
                    q, c = u // NC, u % NC
                    if u < 2:
                        pe.wait_ge(nmrow_ready.sem, nmrow_ready.at(b))
                    else:
                        pe.wait_ge(p_ready.sem, p_ready.at(b, u - 1))
                    for n in range(2):
                        mm = nc.tensor.matmul(psc[u % 2][0:CH, n * 2 * T:(n + 1) * 2 * T],
                                              kp[:, p, 2 * q + n, c * CH:(c + 1) * CH],
                                              qp[:, p, 2 * q + n].rearrange("p h t -> p (h t)"), start=True, stop=True)
                    mm.then_inc(s_mm.sem, 1)
                    if u >= 1:
                        values(b, p, u - 1)
                return step

            def b_gather(b, p):
                values(b, p, QUADS * NC - 1)

            def b_normalize(b, p):
                pe.wait_ge(bo2_ready.sem, bo2_ready.at(b))
                for c in range(4):
                    mm = nc.tensor.transpose(psc[0][0:T, c * 128:c * 128 + 128], bo2[:, c], idn[:])
                mm.then_inc(bot_mm.sem, 1)

            def b_turn(b, p):
                pe.wait_ge(bn_ready.sem, bn_ready.at(b))
                for k in range(KT):
                    mm = nc.tensor.transpose(psc[1][:, k * T:(k + 1) * T], bn[:, k * 128:k * 128 + 128], idn[0:T, 0:T])
                mm.then_inc(bnt_mm.sem, 1)

            def b_output(b, p):
                pe.wait_ge(bnt_ready.sem, bnt_ready.at(b))
                for k in range(KT):
                    mm = nc.tensor.matmul(psc[0][0:T, 0:D], bnt[:, k], wfc[:, k], start=(k == 0), stop=(k == KT - 1))
                mm.then_inc(fc_mm.sem, 1)

            def b_turn_x(b, p):
                pe.wait_ge(x2_ready.sem, x2_ready.at(b))
                for k in range(KT):
                    mm = nc.tensor.transpose(psc[1][:, k * T:(k + 1) * T], x2[:, p, k * 128:k * 128 + 128], idn[0:T, 0:T])
                mm.then_inc(x2t_mm.sem, 1)

            def b_logits(b, p):
                pe.wait_ge(x2l_ready.sem, x2l_ready.at(b))
                if isinstance(b, int) and b == 0:
                    pe.wait_ge(low_weights, 1)
                n = 0
                for xs in (x2l, x2h):
                    for ws in (wr_l, wr_h):
                        for k in range(KT):
                            mm = nc.tensor.matmul(psc[0][0:T, 0:E], xs[:, p, k], ws[:, k], start=(n == 0), stop=(n == 4 * KT - 1))
                            n += 1
                mm.then_inc(lg_mm.sem, 1)

            def c_up(e, half):
                def step(b, p):
                    if half == 0:
                        if e == 0:
                            pe.wait_ge(x2l_ready.sem, x2l_ready.at(b))
                            pe.wait_ge(low_weights, 1 + E)
                        if e >= 2:
                            pe.wait_ge(hd_ready.sem, hd_ready.at(b, e - 1))
                        else:
                            pe.wait_ge(hd_ready.sem, hd_ready.back(b))
                    for m in (2 * half, 2 * half + 1):
                        n = 0
                        for ws, xs in ((wex_l, x2h), (wex_h, x2l), (wex_h, x2h)):
                            for k in range(KT):
                                c = k * 2 * DE + m * 128
                                mm = nc.tensor.matmul(pu[e % 2][:, m * T:(m + 1) * T], ws[:, e, c:c + 128],
                                                      xs[:, p, k], start=(n == 0), stop=(n == 3 * KT - 1))
                                n += 1
                    if half:
                        mm.then_inc(up_mm.sem, 1)
                return step

            def c_down(e):
                def step(b, p):
                    pe.wait_ge(hd_low.sem, hd_low.at(b, e + 1))
                    if e == 0:
                        pe.wait_ge(acc_ready.sem, acc_ready.back(b))
                    else:
                        pe.wait_ge(acc_ready.sem, acc_ready.at(b, e))
                    n = 0
                    for hs, ws in ((hd_l, wex_h), (hd_h, wex_l), (hd_h, wex_h)):
                        for k in range(2):
                            c = KT * 2 * DE + k * D
                            mm = nc.tensor.matmul(pd[0:T, 0:D], hs[:, e % 2, k * T:(k + 1) * T], ws[:, e, c:c + D],
                                                  start=(n == 0), stop=(n == 5))
                            n += 1
                    mm.then_inc(dn_mm.sem, 1)
                return step

            pe.wait_ge(presets, PRESETS)
            pe.wait_ge(vector_presets, 2)
            pipeline(pe, {
                ("A", "qk"): a_qk, ("A", "v"): a_v, ("A", "k_features"): a_k_features, ("A", "q_features"): a_q_features,
                ("A", "kv"): a_kv, ("A", "read"): a_read, ("A", "normalize"): a_normalize, ("A", "turn"): a_turn,
                ("A", "output"): a_output, ("A", "pack"): a_pack,
                ("B", "shift"): b_shift, ("B", "gather"): b_gather, ("B", "normalize"): b_normalize, ("B", "turn"): b_turn,
                ("B", "output"): b_output, ("B", "turn_x"): b_turn_x, ("B", "logits"): b_logits,
            } | {("B", f"max{n}"): b_max(n) for n in range(H // 2)} | {("B", f"unit{u}"): b_unit(u) for u in range(QUADS * NC)}
              | {("C", f"up_{'ab'[h]}{e}"): c_up(e, h) for e in range(E) for h in range(2)}
              | {("C", f"down{e}"): c_down(e) for e in range(E)})

        @block.scalar
        def _(act):
            def a_qk(b, p):
                act.wait_ge(qk_ready.sem, qk_ready.at(b))
                act.wait_ge(qf_mm.sem, qf_mm.back(b))
                nc.scalar.activation(qk[64:128].rearrange("p n t m -> p (n t m)"), qk[0:64].rearrange("p n t m -> p (n t m)"),
                                     ACT.Square).then_inc(squares.sem, 1)

            def a_high(n):
                def step(b, p):
                    act.wait_ge(ctx_in.sem[p], ctx_in.at(b, p))
                    act.wait_ge(s_mm.sem, s_mm.back(b, 2))
                    g = slice(4 * n, 4 * n + 4)
                    nc.scalar.copy(kp[0:96, p, g].rearrange("p g s -> p (g s)"),
                                   kc[:, p, g].rearrange("p g s -> p (g s)")).then_inc(kp_high.sem, 1)
                return step

            def a_k_features(b, p):
                for i in range(2):
                    act.wait_ge(kf_mm.sem, kf_mm.at(b, i + 1))
                    act.wait_ge(kv_mm.sem, kv_mm.back(b))
                    nc.scalar.activation(kf[0:T, i * 512:i * 512 + 512], pa[i][0:T, 0:512], ACT.Exp,
                                         scale=0.5).then_inc(kf_exp.sem, 1)

            def a_q_features(b, p):
                for u in range(2):
                    act.wait_ge(qf_mm.sem, qf_mm.at(b, u + 1))
                    act.wait_ge(ao_mm.sem, ao_mm.back(b))
                    nc.scalar.activation(qf[:, u].rearrange("p t n -> p (t n)"), pa[u][:, 0:4 * T], ACT.Exp,
                                         scale=0.5).then_inc(qf_exp.sem, 1)

            def a_kv(b, p):
                act.wait_ge(kv_mm.sem, kv_mm.at(b))
                act.wait_ge(ao_mm.sem, ao_mm.back(b))
                kv = pa[0][:, 0:PAIRS * 2 * V1].rearrange("p (j d) -> p j d", d=2 * V1)
                nc.scalar.copy(bd[0:64, :, 0:V1], kv[0:64, :, 0:V1]).then_inc(bd_ready.sem, 1)
                nc.scalar.copy(bd[64:128, :, V1:2 * V1], kv[64:128, :, V1:2 * V1]).then_inc(bd_ready.sem, 1)

            def a_read(b, p):
                act.wait_ge(ao_mm.sem, ao_mm.at(b))
                act.wait_ge(aot_mm.sem, aot_mm.back(b))
                nc.scalar.copy(ao[:].rearrange("p c t -> p (c t)"), pa[1][:, 0:4 * T]).then_inc(ao_ready.sem, 1)

            def a_turn(b, p):
                act.wait_ge(ant_mm.sem, ant_mm.at(b))
                act.wait_ge(wo_mm.sem, wo_mm.back(b))
                nc.scalar.copy(ant[:].rearrange("p k t -> p (k t)"), pa[1][:, 0:KT * T]).then_inc(ant_ready.sem, 1)

            def b_shift(b, p):
                for n in range(2):
                    act.wait_ge(nmt_mm.sem, nmt_mm.at(b, n + 1))
                    src = psc[n][:, 0:8 * T // 2].bitcast(F16)
                    nc.scalar.copy(qp[96:97, p, 4 * n:4 * n + 4].rearrange("p g h t -> p (g h t)"),
                                   src[96:97, 0:8 * T]).then_inc(nmrow_ready.sem, 1)

            def b_unit(u):
                def step(b, p):
                    act.wait_ge(s_mm.sem, s_mm.at(b, u + 1))
                    if u >= NP:
                        act.wait_ge(pv_mm.sem, pv_mm.at(b, u - NP + 1))
                    else:
                        act.wait_ge(pv_mm.sem, pv_mm.back(b))
                    nc.scalar.activation(pr[:, u % NP], psc[u % 2][0:CH, 0:4 * T], ACT.Exp,
                                         scale=1.0 / 16.0).then_inc(p_ready.sem, 1)
                return step

            def b_gather(b, p):
                act.wait_ge(pv_mm.sem, pv_mm.at(b))
                act.wait_ge(bot_mm.sem, bot_mm.back(b))
                nc.scalar.copy(bo2[:].rearrange("p c t -> p (c t)"), ppv[:, 0:4 * T]).then_inc(bo2_ready.sem, 1)

            def b_turn(b, p):
                act.wait_ge(bnt_mm.sem, bnt_mm.at(b))
                act.wait_ge(fc_mm.sem, fc_mm.back(b))
                nc.scalar.copy(bnt[:].rearrange("p k t -> p (k t)"), psc[1][:, 0:KT * T]).then_inc(bnt_ready.sem, 1)

            def b_turn_x(b, p):
                act.wait_ge(x2t_mm.sem, x2t_mm.at(b))
                act.wait_ge(up_mm.sem, up_mm.back(b, 2))
                nc.scalar.copy(x2h[:, p].rearrange("p k t -> p (k t)"), psc[1][:, 0:KT * T]).then_inc(x2h_ready.sem, 1)

            def b_logits(b, p):
                act.wait_ge(route.sem, route.at(b, 2))
                nc.scalar.activation(ee[:], m8[:, 0:2], ACT.Exp, bias=nm0[:, 0:1]).then_inc(ee_ready.sem, 1)

            def tanh(b, p, e):
                act.wait_ge(up_mm.sem, up_mm.at(b, e + 1))
                if e >= 2:
                    act.wait_ge(w1_ready.sem, w1_ready.at(b, e - 1))
                else:
                    act.wait_ge(w1_ready.sem, w1_ready.back(b))
                nc.scalar.activation(th[:, e % 2], pu[e % 2][:, 0:2 * T], ACT.Tanh, scale=0.5 / WSCALE).then_inc(th_ready.sem, 1)

            def high(b, p, e):
                act.wait_ge(hd_ready.sem, hd_ready.at(b, e + 1))
                if e >= 2:
                    act.wait_ge(dn_mm.sem, dn_mm.at(b, e - 1))
                else:
                    act.wait_ge(dn_mm.sem, dn_mm.back(b))
                nc.scalar.copy(hd_h[:, e % 2], hd[:, e % 2]).then_inc(hd_high.sem, 1)

            def c_step(*parts):
                def step(b, p):
                    for part, e in parts:
                        part(b, p, e)
                return step

            def c_store(b, p):
                act.wait_ge(y_ready.sem, y_ready.at(b))
                act.dma_start(out[bass.ds(b, 1)].rearrange("o t d -> (o t) d"), yo[:, p]).then_inc(y_out.sem[p], 16)

            def w_split(e):
                if e == 0:
                    act.wait_ge(tail_weights_in, 5 * 16)
                    nc.scalar.mul(wr_h[:].rearrange("p k e -> p (k e)"), wr[:].rearrange("p k e -> p (k e)"),
                                  WSCALE).then_inc(high_weights, 1)
                act.wait_ge(experts_in[e], 16)
                nc.scalar.mul(wex_h[:, e], wex[:, e % NX], WSCALE).then_inc(high_weights, 1)

            act.wait_ge(presets, PRESETS)
            pipeline(act, {
                ("A", "qk"): a_qk, ("A", "high0"): a_high(0), ("A", "high1"): a_high(1), ("A", "k_features"): a_k_features,
                ("A", "q_features"): a_q_features, ("A", "kv"): a_kv, ("A", "read"): a_read, ("A", "turn"): a_turn,
                ("B", "shift"): b_shift, ("B", "gather"): b_gather, ("B", "turn"): b_turn, ("B", "turn_x"): b_turn_x,
                ("B", "logits"): b_logits, ("W", "split"): w_split, ("C", "store"): c_store,
            } | {("B", f"unit{u}"): b_unit(u) for u in range(QUADS * NC)}
              | {("C", "up_b0"): c_step((tanh, 0)), ("C", "up_b1"): c_step((tanh, 1), (high, 0)), ("C", "gap"): c_step((high, E - 1))}
              | {("C", f"up_b{e}"): c_step((tanh, e)) for e in range(2, E)}
              | {("C", f"up_a{e}"): c_step((high, e - 1)) for e in range(2, E)})

        @block.vector
        def _(dve):
            def statistics(b, src, stats, mean_var, st, mv):
                nc.vector.bn_stats(stats[:], src).then_inc(st.sem, 1)
                hold(dve, st.sem, st.at(b))
                nc.vector.bn_aggr(mean_var[0:T], stats[:]).then_inc(mv.sem, 1)

            def normalized(b, src, mean_var, rs, rsr, dst, done):
                dve.wait_ge(rsr.sem, rsr.at(b))
                nc.vector.tensor_scalar(dst, src, mean_var[0:T, 0:1], rs[0:T, 1:2], ALU.subtract, ALU.mult).then_inc(done.sem, 1)

            def a_qk(b, p):
                dve.wait_ge(qk_mm.sem, qk_mm.at(b))
                dve.wait_ge(qf_mm.sem, qf_mm.back(b))
                dst = qk[0:64].rearrange("p n (c w) t -> p (n c) w t", w=2)
                for w in range(2):
                    rows = slice(64 * w, 64 * w + 64)
                    nc.vector.tensor_tensor(dst[:, :, w], pa[0][rows, 0:4 * T].rearrange("p (c t) -> p c t", c=4),
                                            bqk[rows].rearrange("p n c -> p (n c)").unsqueeze(2).to_broadcast([64, 4, T]),
                                            ALU.add).then_inc(qk_ready.sem, 1)

            def a_v(b, p):
                if isinstance(b, int) and b == 0:
                    dve.wait_ge(v_weights_in, 2 * 16)
                dve.wait_ge(v_mm.sem, v_mm.at(b))
                dve.wait_ge(kv_mm.sem, kv_mm.back(b))
                nc.vector.tensor_tensor(v1[:, :, 0:DH], pa[1][0:T, 0:D].rearrange("p (h d) -> p h d", h=H),
                                        bv[:].rearrange("p (h d) -> p h d", h=H), ALU.add).then_inc(v_ready.sem, 1)

            def a_low(n):
                def step(b, p):
                    dve.wait_ge(kp_high.sem, kp_high.at(b, n // 2 + 1))
                    g = slice(2 * n, 2 * n + 2)
                    nc.vector.tensor_tensor(kp[64:96, p, g], kc[64:96, p, g], kp[64:96, p, g],
                                            ALU.subtract).then_inc(kp_low.sem, 1)
                return step

            def a_normalize(b, p):
                dve.wait_ge(aot_mm.sem, aot_mm.at(b))
                sums = pa[0][0:T, 0:512].rearrange("p (j r) -> p j r", j=PAIRS)[:, :, 0:2 * V1].rearrange(
                    "p j (h d) -> p j h d", h=2)
                nc.vector.reciprocal(rda[:].rearrange("p (j h) -> p j h", h=2), sums[:, :, :, DH]).then_inc(rda_ready.sem, 1)
                dve.wait_ge(rda_ready.sem, rda_ready.at(b))
                dve.wait_ge(ant_mm.sem, ant_mm.back(b))
                nc.vector.tensor_tensor(an[:].rearrange("p (j h d) -> p j h d", j=PAIRS, h=2), sums[:, :, :, 0:DH],
                                        rda[:].rearrange("p (j h) -> p j h", h=2).unsqueeze(3).to_broadcast([T, PAIRS, 2, DH]),
                                        ALU.mult).then_inc(an_ready.sem, 1)

            def a_output(b, p):
                dve.wait_ge(wo_mm.sem, wo_mm.at(b))
                dve.wait_ge(xbo_ready.sem, xbo_ready.at(b))
                dve.wait_ge(x1_ready.sem, x1_ready.back(b))
                nc.vector.tensor_tensor(ra[:], pa[0][0:T, 0:D], xbo[0:T], ALU.add).then_inc(ra_ready.sem, 1)
                dve.wait_ge(ra_ready.sem, ra_ready.at(b))
                statistics(b, ra[:], sta, mva, sta_ready, mva_ready)

            def a_apply(b, p):
                normalized(b, ra[:], mva, rsa, rsa_ready, x1[0:T, p], x1_ready)
                x1_v = x1[0:T, p].rearrange("p (g r) -> p g r", g=PAIRS)
                dve.wait_ge(x1_ready.sem, x1_ready.at(b))
                dve.wait_ge(qp_mm.sem, qp_mm.back(b))
                nc.vector.tensor_copy(
                    qs[:, :, 0:128].rearrange("p g (n r) -> p g n r", n=2)[:, :, :, 0:32],
                    x1_v.unsqueeze(2).to_broadcast([T, PAIRS, 2, 32])).then_inc(qs_ready.sem, 1)
                dve.wait_ge(qs_ready.sem, qs_ready.at(b, 1))
                nc.vector.tensor_tensor(qs[:, :, 32:64], x1_v, qs[:, :, 0:32], ALU.subtract).then_inc(qs_ready.sem, 1)

            def a_pack(b, p):
                dve.wait_ge(qp_mm.sem, qp_mm.at(b))
                dve.wait_ge(s_mm.sem, s_mm.back(b, 2))
                src = pa[1][:, 0:PAIRS * T // 2].bitcast(F16).rearrange("p (g t) -> p g t", g=PAIRS)
                for h in range(2):
                    nc.vector.tensor_scalar(qp[:, p, :, h], src, pick[:, h:h + 1], None, ALU.mult).then_inc(qp_ready.sem, 1)

            def b_max(n):
                def step(b, p):
                    for h in (2 * n, 2 * n + 1):
                        dve.wait_ge(max_mm.sem, max_mm.at(b, h + 1))
                        if h == 0:
                            dve.wait_ge(nm_ready.sem, nm_ready.back(b))
                        nc.vector.tensor_reduce(mx[:, h:h + 1], psc[h % 2][0:T, 0:S2], AX_X, ALU.max).then_inc(max_ready.sem, 1)
                return step

            def b_shift(b, p):
                dve.wait_ge(max_ready.sem, max_ready.at(b))
                dve.wait_ge(nmt_mm.sem, nmt_mm.back(b))
                nc.vector.tensor_scalar(nm[:], mx[:], -1.0 / SHIFT, None, ALU.mult).then_inc(nm_ready.sem, 1)

            def b_normalize(b, p):
                dve.wait_ge(bot_mm.sem, bot_mm.at(b))
                sums = psc[0][0:T, 0:512].rearrange("p (h r) -> p h r", h=H)
                nc.vector.reciprocal(rdb[:].unsqueeze(2), sums[:, :, DH:V1]).then_inc(rdb_ready.sem, 1)
                dve.wait_ge(rdb_ready.sem, rdb_ready.at(b))
                dve.wait_ge(bnt_mm.sem, bnt_mm.back(b))
                nc.vector.tensor_tensor(bn[:].rearrange("p (h d) -> p h d", h=H), sums[:, :, 0:DH],
                                        rdb[:].unsqueeze(2).to_broadcast([T, H, DH]), ALU.mult).then_inc(bn_ready.sem, 1)

            def b_output(b, p):
                dve.wait_ge(fc_mm.sem, fc_mm.at(b))
                dve.wait_ge(x1b_ready.sem, x1b_ready.at(b))
                dve.wait_ge(x2_ready.sem, x2_ready.back(b))
                nc.vector.tensor_tensor(rb[:], psc[0][0:T, 0:D], x1b[0:T], ALU.add).then_inc(rb_ready.sem, 1)
                dve.wait_ge(rb_ready.sem, rb_ready.at(b))
                statistics(b, rb[:], stb, mvb, stb_ready, mvb_ready)

            def b_apply(b, p):
                normalized(b, rb[:], mvb, rsb, rsb_ready, x2[:, p], x2_ready)

            def b_turn_x(b, p):
                dve.wait_ge(x2h_ready.sem, x2h_ready.at(b))
                nc.vector.tensor_tensor(x2l[:, p].rearrange("p k t -> p (k t)"), psc[1][:, 0:KT * T],
                                        x2h[:, p].rearrange("p k t -> p (k t)"), ALU.subtract).then_inc(x2l_ready.sem, 1)

            def b_logits(b, p):
                dve.wait_ge(lg_mm.sem, lg_mm.at(b))
                nc.vector.tensor_scalar(lg[:], psc[0][0:T, 0:E], 1.0 / WSCALE, None, ALU.mult).then_inc(lg_ready.sem, 1)
                hold(dve, lg_ready.sem, lg_ready.at(b))
                nc.vector.max(m8[:], lg[:]).then_inc(route.sem, 1)
                dve.wait_ge(route.sem, route.at(b, 1))
                nc.vector.tensor_scalar(nm0[:], m8[:, 0:1], -1.0, None, ALU.mult).then_inc(route.sem, 1)
                nc.vector.max_index(i8[:], m8[:], lg[:]).then_inc(route.sem, 1)
                dve.wait_ge(route.sem, route.at(b, 3))
                nc.vector.tensor_copy(i8f[:], i8[:, 0:2]).then_inc(route.sem, 1)
                dve.wait_ge(ee_ready.sem, ee_ready.at(b))
                nc.vector.tensor_tensor(es[:], ee[:, 0:1], ee[:, 1:2], ALU.add).then_inc(route.sem, 1)
                dve.wait_ge(route.sem, route.at(b, 5))
                nc.vector.reciprocal(er[:], es[:]).then_inc(route.sem, 1)
                dve.wait_ge(route.sem, route.at(b, 6))
                nc.vector.tensor_scalar(gg[:], ee[:], er[:, 0:1], 0.5 / WSCALE, ALU.mult, ALU.mult).then_inc(route.sem, 1)
                dve.wait_ge(route.sem, route.at(b, 7))
                for n in range(2):
                    last = nc.vector.tensor_scalar(g01[:, n], pick[0:T, 2:2 + E], i8f[:, n:n + 1], gg[:, n:n + 1],
                                                   ALU.is_equal, ALU.mult)
                last.then_inc(route.sem, 1)
                dve.wait_ge(route.sem, route.at(b, 8))
                nc.vector.tensor_tensor(gate[:, p], g01[:, 0], g01[:, 1], ALU.add).then_inc(gate_ready.sem, 1)

            def gated(b, p, e):
                dve.wait_ge(dn_mm.sem, dn_mm.at(b, e + 1))
                if e == 0:
                    dve.wait_ge(gate_ready.sem, gate_ready.at(b))
                    dve.wait_ge(y_ready.sem, y_ready.back(b))
                    prev = x2[:, p]
                else:
                    dve.wait_ge(acc_ready.sem, acc_ready.at(b, e))
                    prev = acc[:, (e - 1) % 2]
                nc.vector.scalar_tensor_tensor(out=acc[:, e % 2], in0=pd[0:T, 0:D], scalar=gate[:, p, e:e + 1], in1=prev,
                                               op0=ALU.mult, op1=ALU.add).then_inc(acc_ready.sem, 1)

            def hidden(b, p, e):
                dve.wait_ge(th_ready.sem, th_ready.at(b, e + 1))
                if e >= 2:
                    dve.wait_ge(hd_ready.sem, hd_ready.at(b, e - 1))
                else:
                    dve.wait_ge(hd_ready.sem, hd_ready.back(b))
                nc.vector.scalar_tensor_tensor(out=w1[:, e % 2], in0=th[:, e % 2], scalar=1.0, in1=pu[e % 2][:, 0:2 * T],
                                               op0=ALU.add, op1=ALU.mult).then_inc(w1_ready.sem, 1)
                dve.wait_ge(w1_ready.sem, w1_ready.at(b, e + 1))
                if e >= 2:
                    dve.wait_ge(hd_low.sem, hd_low.at(b, e - 1))
                else:
                    dve.wait_ge(hd_low.sem, hd_low.back(b))
                nc.vector.scalar_tensor_tensor(out=hd[:, e % 2], in0=w1[:, e % 2], scalar=1.0 / WSCALE ** 2,
                                               in1=pu[e % 2][:, 2 * T:4 * T], op0=ALU.mult, op1=ALU.mult).then_inc(hd_ready.sem, 1)

            def c_step(*parts):
                def step(b, p):
                    for part, e in parts:
                        part(b, p, e)
                return step

            def c_finish(b, p):
                gated(b, p, E - 1)
                dve.wait_ge(acc_ready.sem, acc_ready.at(b))
                statistics(b, acc[:, (E - 1) % 2], stc, mvc, stc_ready, mvc_ready)

            def c_store(b, p):
                dve.wait_ge(y_out.sem[p], y_out.back(b, p))
                normalized(b, acc[:, (E - 1) % 2], mvc, rsc, rsc_ready, yo[:, p], y_ready)

            def w_split(e):
                if e == 0:
                    dve.wait_ge(high_weights, 1)
                    nc.vector.scalar_tensor_tensor(out=wr_l[:].rearrange("p k e -> p (k e)"), in0=wr[:].rearrange("p k e -> p (k e)"),
                                                   scalar=WSCALE, in1=wr_h[:].rearrange("p k e -> p (k e)"),
                                                   op0=ALU.mult, op1=ALU.subtract).then_inc(low_weights, 1)
                dve.wait_ge(high_weights, e + 2)
                nc.vector.scalar_tensor_tensor(out=wex_l[:, e], in0=wex[:, e % NX], scalar=WSCALE, in1=wex_h[:, e],
                                               op0=ALU.mult, op1=ALU.subtract).then_inc(low_weights, 1)

            dve.wait_ge(mask_in, 16)
            nc.vector.tensor_scalar(mask_h[:], mask_i[:], 0.0, -BIG, ALU.is_equal, ALU.mult).then_inc(mask_ready, 1)
            nc.vector.memset(ppv[:], 0.0).then_inc(vector_presets, 1)
            nc.vector.memset(v1[:, :, DH:V1], 1.0).then_inc(vector_presets, 1)
            dve.wait_ge(consts_in, 2 * 16)
            nc.vector.tensor_copy(idh[:], idn[:]).then_inc(ident_ready, 1)
            dve.wait_ge(presets, PRESETS)
            dve.wait_ge(qk_weights_in, 4 * 16)
            pipeline(dve, {
                ("A", "qk"): a_qk, ("A", "v"): a_v, ("A", "normalize"): a_normalize, ("A", "output"): a_output,
                ("A", "apply"): a_apply, ("A", "pack"): a_pack,
                ("B", "shift"): b_shift, ("B", "normalize"): b_normalize, ("B", "output"): b_output, ("B", "apply"): b_apply,
                ("B", "turn_x"): b_turn_x, ("B", "logits"): b_logits, ("W", "split"): w_split,
                ("C", "finish"): c_finish, ("C", "store"): c_store,
            } | {("A", f"low{n}"): a_low(n) for n in range(4)} | {("B", f"max{n}"): b_max(n) for n in range(H // 2)}
              | {("C", "up_a1"): c_step((hidden, 0)), ("C", "gap"): c_step((gated, E - 2))}
              | {("C", f"down{e - 1}"): c_step((hidden, e)) for e in range(1, E)}
              | {("C", f"up_a{e + 2}"): c_step((gated, e)) for e in range(E - 2)})

        @block.gpsimd
        def _(pool):
            def inverse_root(b, mv, mean_var, rs, rsr):
                hold(pool, mv.sem, mv.at(b))
                nc.gpsimd.tensor_scalar(rs[:, 0:1], mean_var[:, 1:2], LN_EPS, 1.0, ALU.add, ALU.mult).then_inc(rsr.sem, 1)
                pool.wait_ge(rsr.sem, rsr.at(b, 1))
                nc.gpsimd.tensor_tensor(rs[:, 1:2], rs[:, 0:1], pick[:, 2 + E:3 + E], ALU.pow).then_inc(rsr.sem, 1)

            def a_k_features(b, p):
                for i in range(2):
                    hold(pool, kf_exp.sem, kf_exp.at(b, i + 1))
                    nc.gpsimd.tensor_scalar(kf[:, i * 512:i * 512 + 512], kf[:, i * 512:i * 512 + 512], FEATURE_EPS, 1.0,
                                            ALU.add, ALU.mult).then_inc(kf_ready.sem, 1)

            def a_q_features(b, p):
                for u in range(2):
                    hold(pool, qf_exp.sem, qf_exp.at(b, u + 1))
                    nc.gpsimd.tensor_scalar(qf[:, u], qf[:, u], FEATURE_EPS, 1.0, ALU.add, ALU.mult).then_inc(qf_ready.sem, 1)

            def a_kv(b, p):
                pool.wait_ge(x_in.sem[p], x_in.at(b, p))
                pool.wait_ge(ra_ready.sem, ra_ready.back(b))
                if isinstance(b, int) and b == 0:
                    pool.wait_ge(tail_weights_in, 5 * 16)
                nc.gpsimd.tensor_tensor(xbo[:], xr[:, p], bo[:], ALU.add).then_inc(xbo_ready.sem, 1)

            def a_output(b, p):
                inverse_root(b, mva_ready, mva, rsa, rsa_ready)

            def b_shift(b, p):
                pool.wait_ge(x1_ready.sem, x1_ready.at(b))
                pool.wait_ge(rb_ready.sem, rb_ready.back(b))
                nc.gpsimd.tensor_tensor(x1b[:], x1[:, p], bfc[:], ALU.add).then_inc(x1b_ready.sem, 1)

            def b_output(b, p):
                inverse_root(b, mvb_ready, mvb, rsb, rsb_ready)

            def low(e):
                def step(b, p):
                    pool.wait_ge(hd_high.sem, hd_high.at(b, e + 1))
                    if e >= 2:
                        pool.wait_ge(dn_mm.sem, dn_mm.at(b, e - 1))
                    else:
                        pool.wait_ge(dn_mm.sem, dn_mm.back(b))
                    nc.gpsimd.tensor_tensor(hd_l[:, e % 2], hd[:, e % 2], hd_h[:, e % 2], ALU.subtract).then_inc(hd_low.sem, 1)
                return step

            def c_finish(b, p):
                inverse_root(b, mvc_ready, mvc, rsc, rsc_ready)

            for n, (ap, value) in enumerate((
                    (xr[96:128], 0.0), (kf[96:128], 0.0), (bo[96:128], 0.0), (bfc[96:128], 0.0), (x1[96:128], 0.0),
                    (mva[:], 1.0), (mvb[:], 1.0), (mvc[:], 1.0), (bd[:], 0.0), (qs[:, :, 96:128], 0.0),
                    (kp[96:128], 0.0), (qs[:, :, 97:98], BIG), (kp[96:97], SHIFT))):
                if n:
                    pool.wait_ge(presets, n)
                nc.gpsimd.memset(ap, value).then_inc(presets, 1)
            pool.wait_ge(presets, PRESETS)
            pool.wait_ge(consts_in, 2 * 16)
            pipeline(pool, {
                ("A", "k_features"): a_k_features, ("A", "q_features"): a_q_features, ("A", "kv"): a_kv,
                ("A", "output"): a_output, ("B", "shift"): b_shift, ("B", "output"): b_output, ("C", "finish"): c_finish,
                ("C", "up_b1"): low(0), ("C", "gap"): low(E - 1),
            } | {("C", f"up_a{e + 1}"): low(e) for e in range(1, E - 1)})


def kernel(**inputs):
    import numpy as np
    import concourse.bacc as bacc
    from concourse.bass_utils import run_bass_kernel_spmd

    f = {n: np.asarray(a) for n, a in inputs.items()}
    x, c = f["x"], f["ctx_1024"]

    def rows128(w):
        return w.reshape(-1, 128, w.shape[-1]).transpose(1, 0, 2)

    def every_token(v):
        return np.broadcast_to(v, (T, D))

    orf_rows = np.zeros((128, 4, M), np.float32)
    for h in range(4):
        orf_rows[h * DH:(h + 1) * DH, h] = f["L0_attn_orf"].T
        orf_rows[64 + h * DH:64 + (h + 1) * DH, h] = -0.25
    picks = np.zeros((128, 2 + E + 1), np.float32)
    for p in range(128):
        picks[p, 0] = p >= 96 or p % 32 < DH
        picks[p, 1] = p >= 96 or p % 32 >= DH
    picks[:, 2:2 + E] = np.arange(E)
    picks[:, 2 + E] = -0.5
    values = np.ones((B, CH, NC, H, V1), np.float32)
    values[..., :DH] = c.reshape(B, NC, CH, H, DH).transpose(0, 2, 1, 3, 4)

    arrays = {
        "x_rows": x,
        "x_cols": x.transpose(0, 2, 1).reshape(B, KT, 128, T).transpose(0, 2, 1, 3),
        "ctx_cols": c.transpose(0, 2, 1).reshape(B, PAIRS, 32, S2).transpose(0, 2, 1, 3),
        "ctx_rows": values,
        "mask": f["mask_Bx1x1xS2_ik0"].reshape(1, B * S2).astype(np.int32),
        "w_q": rows128(f["L0_attn_Wq"].T), "w_k": rows128(f["L0_attn_Wk"].T),
        "w_v": rows128(f["L0_attn_Wv"].T), "w_o": rows128(f["L0_attn_Wo"].T), "w_fc": rows128(f["L0_xattn_fc_w"].T),
        "b_qk": np.stack([f["L0_attn_bq"].reshape(KT, 128).T, f["L0_attn_bk"].reshape(KT, 128).T], 1),
        "b_v": every_token(f["L0_attn_bv"]), "b_o": every_token(f["L0_attn_bo"]), "b_fc": every_token(f["L0_xattn_fc_b"]),
        "orf_rows": orf_rows.reshape(128, 4 * M),
        "w_router": rows128(f["L0_ffn_router_w"].T),
        "w_experts": np.concatenate([
            f["L0_ffn_up_proj"].reshape(E, KT, 128, 2 * DE).transpose(2, 0, 1, 3).reshape(128, E, KT * 2 * DE),
            f["L0_ffn_down_proj"].reshape(E, DE // 128, 128, D).transpose(2, 0, 1, 3).reshape(128, E, DE // 128 * D)], 2),
        "ident": np.eye(128, dtype=np.float32),
        "picks": picks,
    }
    nc = bacc.Bacc("TRN2", target_bir_lowering=False, num_devices=1)
    feeds, args = {}, {}
    for name, a in arrays.items():
        a = np.ascontiguousarray(a)
        feeds[f"in_{name}"] = a
        args[name] = nc.dram_tensor(f"in_{name}", a.shape, mybir.dt.from_np(a.dtype), kind="ExternalInput").ap()
    args["out"] = nc.dram_tensor("out", (B, T, D), F32, kind="ExternalOutput").ap()
    build(nc, **args)
    r = run_bass_kernel_spmd(nc, [feeds], core_ids=[0])
    return r.results[0]["out"]
```

```python
from contextlib import ExitStack

import concourse.bass as bass
from concourse import mybir

F32 = mybir.dt.float32
F16 = mybir.dt.float16
I32 = mybir.dt.int32
U32 = mybir.dt.uint32
ACT = mybir.ActivationFunctionType
ALU = mybir.AluOpType
AX_X = mybir.AxisListType.X

B, T, D = 8, 112, 256
S2, CH = 375, 125
NC = S2 // CH
H, DH, M = 16, 16, 64
KT = D // 128
E, DE = 8, 256
PAIRS = H // 2
QUADS = H // 4
V1 = DH + 1
FEATURE_EPS = 1e-6
LN_EPS = 1e-5
SHIFT = 64.0
BIG = 60000.0

WSCALE = 64.0
VALUE_PARTS = (KT * D, D)
TAIL_PARTS = (KT * D, D, KT * D, D, KT * E)
SMALL_PARTS = (2 * KT, 4 * M, 128, 2 + E + 1)

EXPERTS = (["up_a0", "up_b0", "up_a1", "up_b1"]
           + [f"{s}{e - 2 * (s == 'down')}" for e in range(2, E) for s in ("up_a", "up_b", "down")]
           + [f"down{E - 2}", f"down{E - 1}"])
VECTOR = (["hidden0", "hidden1", "hidden2"] + [f"{s}{e - 3 * (s == 'gated')}" for e in range(3, E) for s in ("gated", "hidden")]
          + [f"gated{E - 3}", f"gated{E - 2}", "finish", "store"])
SPLITS = [f"split{e}" for e in range(E)]

FIRST = """
    A.qk A.v A.k_features A.q_features A.kv A.high0 A.read A.high1 A.normalize A.turn A.output A.low0 A.apply A.low1
    A.low2 A.pack A.low3
"""
SECOND = """
    B.max0 W.0 A.qk B.max1 B.max2 A.v W.1 B.max3 W.2 A.k_features A.q_features B.max4 B.max5 B.max6 A.high0 B.max7
    B.shift A.kv B.unit0 W.3 B.unit1 A.read B.unit2 A.low0 B.unit3 B.unit4 B.unit5 A.high1 A.normalize A.turn
    A.output W.4 A.low1 B.unit6 B.unit7 B.unit8 A.low2 B.unit9 B.unit10 B.unit11 A.apply B.gather B.normalize W.5
    B.turn A.low3 B.output A.pack B.apply B.turn_x B.logits W.6 W.7
"""
MAIN = """
    B.max0 C.route1 A.qk B.max1 C.route2 C B.max2 C.route3 A.v B.max3 C.route4 C A.k_features V B.max4 C.route5 C
    B.max5 C.route6 H C B.max6 C.route7 V A.q_features B.max7 A.high0 C C H B.shift A.kv V C C H V B.unit0 A.read
    B.unit1 C B.unit2 B.unit3 B.unit4 A.low0 A.high1 C V V A.normalize B.unit5 H A.low1 C B.unit6 A.turn B.unit7
    A.output A.low2 B.unit8 C C A.low3 V B.unit9 V C B.unit10 B.unit11 H B.gather A.apply C B.normalize V C B.turn C
    H A.pack V B.output C C C H V V B.apply C V V C B.turn_x C V H B.logits C V V
"""
DRAIN = """
    C B.max0 C.route1 B.max1 C.route2 B.max2 C.route3 C B.max3 C.route4 C V B.max4 C.route5 C H B.max5 C.route6 C H
    V B.max6 C.route7 C C B.max7 B.shift V V C H C C B.unit0 B.unit1 B.unit2 B.unit3 V B.unit4 C B.unit5 V B.unit6 H
    C B.unit7 B.unit8 B.unit9 B.unit10 B.unit11 C V B.gather V C H B.normalize V C C V B.turn H C B.output V V C C C
    H C B.apply C V V B.turn_x C H C V V V B.logits
"""
LAST = """
    C.route1 C.route2 V C C.route3 C.route4 C.route5 C.route6 C.route7 C H C C V H C C C V C H C V C V C C V C V H C
    V H C V H V V C C C C V C C C H V V H V V C V C
"""


def order(text):
    lists = {"C": iter(EXPERTS), "V": iter(VECTOR), "H": iter(SPLITS)}
    return [("C", next(lists[s])) if s in lists else tuple(s.split(".")) for s in text.split()]


LAG = {"W": 0, "A": 0, "B": 1, "C": 2}


class Count:

    def __init__(self, nc, ctx, name, per=1):
        self.sem = ctx.enter_context(nc.semaphore(name))
        self.per = per
        nc.scalar.sem_inc(self.sem, 2 * self.per)

    def at(self, b, k=None):
        return b * self.per + (2 * self.per + (self.per if k is None else k))

    def back(self, b, depth=1):
        return b * self.per + (3 - depth) * self.per


class Landing:

    def __init__(self, nc, ctx, name):
        self.sem = [ctx.enter_context(nc.semaphore(f"{name}{p}")) for p in range(2)]
        for s in self.sem:
            nc.scalar.sem_inc(s, 16)

    def at(self, b, p):
        return (b - p) * 8 + 32

    def back(self, b, p):
        return (b - p) * 8 + 16


def build(nc, x_both, ctx_cols, ctx_rows, mask, w_q, w_k, w_v, w_tail, w_experts, consts, out):
    with ExitStack() as ctx:
        def sb(name, shape, dt=F32):
            return ctx.enter_context(nc.sbuf_tensor(name, shape, dt))

        def bank(name):
            return ctx.enter_context(nc.psum_tensor(name, [128, 512], F32))

        def sem(name):
            return ctx.enter_context(nc.semaphore(name))

        wqk = sb("wqk", [128, 2, KT, D])

        def parts(whole, widths):
            ends = [sum(widths[:n + 1]) for n in range(len(widths))]
            assert ends[-1] == whole.shape[1]
            return [whole[:, end - w:end] for end, w in zip(ends, widths)]

        def tiles(ap):
            return ap.rearrange("p (k d) -> p k d", k=KT)

        values_in = sb("values_in", [128, sum(VALUE_PARTS)])
        wv, bv = parts(values_in, VALUE_PARTS)
        tail_in = sb("tail_in", [128, sum(TAIL_PARTS)])
        wo, bo, wfc, bfc, wr = parts(tail_in, TAIL_PARTS)
        wv, wo, wfc, wr = tiles(wv), tiles(wo), tiles(wfc), tiles(wr)
        small_in = sb("small_in", [128, sum(SMALL_PARTS)])
        bqk, orf, idn, pick = parts(small_in, SMALL_PARTS)
        wr_h, wr_l = sb("wr_h", [128, KT, E], F16), sb("wr_l", [128, KT, E], F16)
        EW = KT * 2 * DE + DE // 128 * D
        NX = 3
        wex = sb("wex", [128, NX, EW])
        wex_h, wex_l = sb("wex_h", [128, E, EW], F16), sb("wex_l", [128, E, EW], F16)
        idh = sb("idh", [128, 128], F16)
        mask_i = sb("mask_i", [1, B * S2], I32)
        mask_h = sb("mask_h", [1, B * S2], F16)

        x_both_in = sb("x_both_in", [128, 2, KT * T + D])
        xc = x_both_in[:, :, 0:KT * T].rearrange("p n (k t) -> p n k t", k=KT)
        xr = x_both_in[:, :, KT * T:KT * T + D]
        xbo = sb("xbo", [128, D])
        qk = sb("qk", [128, 2, 4, T])
        v1 = sb("v1", [T, H, V1])
        kf = sb("kf", [128, H * M])
        qf = sb("qf", [128, 2, 4, T])
        bd = sb("bd", [128, PAIRS, 64])
        ao = sb("ao", [128, 4, T])
        rda = sb("rda", [T, H])
        an = sb("an", [T, D])
        ant = sb("ant", [128, KT, T])
        ra = sb("ra", [T, D])
        sta = sb("sta", [T, 6])
        mva = sb("mva", [128, 2])
        rsa = sb("rsa", [128, 2])
        x1 = sb("x1", [128, 2, D])
        qs = sb("qs", [T, PAIRS, 128], F16)
        qp = sb("qp", [128, 2, PAIRS, 2, T], F16)

        kc = sb("kc", [96, 2, PAIRS, S2])
        kp_all = sb("kp", [128, 2 * PAIRS * S2], F16)
        kp = kp_all[:].rearrange("p (n g s) -> p n g s", n=2, g=PAIRS)
        vx = sb("vx", [CH, 2, NC, H, V1])
        x1b = sb("x1b", [128, D])
        mx = sb("mx", [T, H])
        nm = sb("nm", [T, H], F16)
        NP = 4
        pr = sb("pr", [CH, NP, 4 * T])
        bo2 = sb("bo2", [128, QUADS, T])
        rdb = sb("rdb", [T, H])
        bn = sb("bn", [T, D])
        bnt = sb("bnt", [128, KT, T])
        rb = sb("rb", [T, D])
        stb = sb("stb", [T, 6])
        mvb = sb("mvb", [128, 2])
        rsb = sb("rsb", [128, 2])
        x2 = sb("x2", [T, 2, D])
        x2h, x2l = sb("x2h", [128, 2, KT, T], F16), sb("x2l", [128, 2, KT, T], F16)
        lg = sb("lg", [T, E])
        m8 = sb("m8", [T, 8])
        i8 = sb("i8", [T, 8], U32)
        i8f = sb("i8f", [T, 2])
        nm0 = sb("nm0", [T, 1])
        ee = sb("ee", [T, 2])
        es = sb("es", [T, 1])
        er = sb("er", [T, 1])
        gg = sb("gg", [T, 2])
        g01 = sb("g01", [T, 2, E])
        gate = sb("gate", [T, 2, E])

        th = sb("th", [128, 2, 2 * T])
        w1 = sb("w1", [128, 2, 2 * T])
        hd = sb("hd", [128, 2, 2 * T])
        NH = 4
        hd_h, hd_l = sb("hd_h", [128, NH, 2 * T], F16), sb("hd_l", [128, NH, 2 * T], F16)
        acc = sb("acc", [T, 2, D])
        stc = sb("stc", [T, 6])
        mvc = sb("mvc", [128, 2])
        rsc = sb("rsc", [128, 2])
        yo = sb("yo", [T, 2, D])

        pa = [bank("pa0"), bank("pa1")]
        psc = [bank("ps0"), bank("ps1")]
        ppv = bank("ppv")
        pu = [bank("pu0"), bank("pu1")]
        pd = bank("pd")

        q_weights_in, k_weights_in = sem("q_weights_in"), sem("k_weights_in")
        v_weights_in, consts_in = sem("v_weights_in"), sem("consts_in")
        tail_weights_in = sem("tail_weights_in")
        experts_in = [sem(f"experts_in{e}") for e in range(E)]
        high_weights, low_weights = sem("high_weights"), sem("low_weights")
        mask_in = sem("mask_in")
        mask_ready = sem("mask_ready")
        ident_ready = sem("ident_ready")
        vector_presets = sem("vector_presets")
        presets = sem("presets")

        def count(name, per=1):
            return Count(nc, ctx, name, per)

        x_in, ctx_in = Landing(nc, ctx, "x_in"), Landing(nc, ctx, "ctx_in")
        v_in, mrow_in = Landing(nc, ctx, "v_in"), Landing(nc, ctx, "mrow_in")
        y_out = Landing(nc, ctx, "y_out")
        qk_mm, v_mm = count("qk_mm"), count("v_mm")
        qk_ready, v_ready = count("qk_ready", 2), count("v_ready")
        squares = count("squares")
        kf_mm, qf_mm = count("kf_mm", 2), count("qf_mm", 2)
        kf_exp, qf_exp = count("kf_exp", 2), count("qf_exp", 2)
        kf_ready, qf_ready = count("kf_ready", 2), count("qf_ready", 2)
        kv_mm, bd_ready = count("kv_mm"), count("bd_ready", 2)
        ao_mm, ao_ready = count("ao_mm"), count("ao_ready")
        aot_mm, rda_ready, an_ready = count("aot_mm"), count("rda_ready"), count("an_ready")
        ant_mm, ant_ready = count("ant_mm"), count("ant_ready")
        wo_mm, xbo_ready, ra_ready = count("wo_mm"), count("xbo_ready"), count("ra_ready")
        sta_ready, mva_ready, rsa_ready = count("sta_ready"), count("mva_ready"), count("rsa_ready", 2)
        x1_ready, qs_ready = count("x1_ready"), count("qs_ready", 2)
        qp_mm, qp_ready = count("qp_mm", 2), count("qp_ready", 4)
        kp_high, kp_low = count("kp_high", 2), count("kp_low", 4)
        max_mm, max_ready = count("max_mm", H), count("max_ready", H)
        nm_ready, nmt_mm, nmrow_ready = count("nm_ready"), count("nmt_mm", 2), count("nmrow_ready", 2)
        s_mm, p_ready, pv_mm = count("s_mm", QUADS * NC), count("p_ready", QUADS * NC), count("pv_mm", QUADS * NC)
        bo2_ready, bot_mm = count("bo2_ready"), count("bot_mm")
        rdb_ready, bn_ready = count("rdb_ready"), count("bn_ready")
        bnt_mm, bnt_ready, fc_mm = count("bnt_mm"), count("bnt_ready"), count("fc_mm")
        x1b_ready, rb_ready, stb_ready = count("x1b_ready"), count("rb_ready"), count("stb_ready")
        mvb_ready, rsb_ready, x2_ready = count("mvb_ready"), count("rsb_ready", 2), count("x2_ready")
        x2t_mm, x2h_ready, x2l_ready, lg_mm, lg_ready = count("x2t_mm"), count("x2h_ready"), count("x2l_ready"), count("lg_mm"), count("lg_ready")
        route = count("route", 8)
        ee_ready, gate_ready = count("ee_ready"), count("gate_ready")
        hd_high, hd_low = count("hd_high", E), count("hd_low", E)
        up_mm, th_ready, w1_ready, hd_ready = (count(n, E) for n in ("up_mm", "th_ready", "w1_ready", "hd_ready"))
        dn_mm, acc_ready = count("dn_mm", E), count("acc_ready", E)
        stc_ready, mvc_ready, rsc_ready = count("stc_ready"), count("mvc_ready"), count("rsc_ready", 2)
        y_ready = count("y_ready")

        waited = sem("waited")

        def hold(eng, sem_, value):
            eng.wait_ge(sem_, value)
            eng.sem_inc(waited, 1)

        shift_row = sem("shift_row")
        PRESETS, VECTOR_PRESETS = 8, 3

        block = ctx.enter_context(nc.Block())

        def iteration(steps, text, i, half):
            for stage, step in order(text):
                if (stage, step) in steps:
                    steps[stage, step](i - LAG[stage], (half - LAG[stage]) % 2)

        def pipeline(eng, steps):
            iteration(steps, FIRST, 0, 0)
            iteration(steps, SECOND, 1, 1)
            with eng.Fori(2, B - 1, 2) as i:
                iteration(steps, MAIN, i, 0)
                iteration(steps, MAIN, i + 1, 1)
            iteration(steps, DRAIN, B, B % 2)
            iteration(steps, LAST, B + 1, (B + 1) % 2)

        @block.sync
        def _(sp):
            def load_x(b, p):
                if not isinstance(b, int):
                    sp.wait_ge(xbo_ready.sem, xbo_ready.back(b, 2))
                    sp.wait_ge(v_mm.sem, v_mm.back(b, 2))
                sp.dma_start(x_both_in[:, p], x_both[bass.ds(b, 1)].rearrange("o p x -> (o p) x")).then_inc(x_in.sem[p], 16)

            def load_context(b, p):
                sp.wait_ge(kp_low.sem, kp_low.back(b, 2))
                sp.dma_start(kc[:, p], ctx_cols[bass.ds(b, 1)].to_broadcast([3, 32, PAIRS, S2]).rearrange("n r g s -> n r (g s)")).then_inc(ctx_in.sem[p], 16)
                sp.wait_ge(pv_mm.sem, pv_mm.back(b, 2))
                sp.dma_start(vx[:, p], ctx_rows[bass.ds(b, 1)].rearrange("o s c h v -> (o s) c h v")).then_inc(v_in.sem[p], 16)
                sp.wait_ge(s_mm.sem, s_mm.back(b, 2))
                sp.dma_start(kp[97:98, p], mask_h[0:1, bass.ds(b * S2, S2)].rearrange("o (u s) -> o u s", u=1).to_broadcast([1, PAIRS, S2])).then_inc(mrow_in.sem[p], 16)

            load_x(0, 0)
            for dst, src, done in (
                    (wqk[:, 0], w_q, q_weights_in), (wqk[:, 1], w_k, k_weights_in), (small_in[:], consts, consts_in),
                    (values_in[:], w_v, v_weights_in), (mask_i[:], mask, mask_in)):
                sp.dma_start(dst, src).then_inc(done, 16)
            sp.wait_ge(mask_ready, 1)
            sp.wait_ge(vector_presets, VECTOR_PRESETS)
            load_context(0, 0)
            sp.dma_start(tail_in[:], w_tail).then_inc(tail_weights_in, 16)
            for e in range(2):
                sp.dma_start(wex[:, e % NX], w_experts[:, e]).then_inc(experts_in[e], 16)
            load_x(1, 1)
            load_context(1, 1)
            for e in range(2, E):
                if e >= NX:
                    sp.wait_ge(low_weights, 1 + e - NX + 1)
                sp.dma_start(wex[:, e % NX], w_experts[:, e]).then_inc(experts_in[e], 16)
            with sp.Fori(2, B - 1, 2) as b:
                load_x(b, 0)
                load_context(b, 0)
                load_x(b + 1, 1)
                load_context(b + 1, 1)
            for b in (B - 2, B - 1):
                sp.wait_ge(y_out.sem[b % 2], y_out.at(b, b % 2))

        @block.tensor
        def _(pe):
            def a_qk(b, p):
                first = isinstance(b, int) and b == 0
                pe.wait_ge(x_in.sem[p], x_in.at(b, p))
                pe.wait_ge(qp_ready.sem, qp_ready.back(b))
                for n in range(2):
                    if first:
                        pe.wait_ge((q_weights_in, k_weights_in)[n], 16)
                    for c in range(KT):
                        for k in range(KT):
                            mm = nc.tensor.matmul(pa[0][:, (n * KT + c) * T:(n * KT + c + 1) * T],
                                                  wqk[:, n, k, c * 128:c * 128 + 128], xc[:, p, k],
                                                  start=(k == 0), stop=(k == KT - 1))
                mm.then_inc(qk_mm.sem, 1)

            def a_v(b, p):
                if isinstance(b, int) and b == 0:
                    pe.wait_ge(v_weights_in, 16)
                for k in range(KT):
                    mm = nc.tensor.matmul(pa[1][0:T, 0:D], xc[:, p, k], wv[:, k], start=(k == 0), stop=(k == KT - 1))
                mm.then_inc(v_mm.sem, 1)

            def a_k_features(b, p):
                if isinstance(b, int) and b == 0:
                    pe.wait_ge(consts_in, 16)
                pe.wait_ge(squares.sem, squares.at(b))
                for i in range(2):
                    if i == 1:
                        pe.wait_ge(v_ready.sem, v_ready.at(b))
                    for t in (2 * i, 2 * i + 1):
                        mm = nc.tensor.matmul(pa[i][0:T, (t % 2) * 256:(t % 2) * 256 + 256], qk[:, 1, t], orf,
                                              start=True, stop=True)
                    mm.then_inc(kf_mm.sem, 1)

            def a_q_features(b, p):
                for u in range(2):
                    pe.wait_ge(kf_exp.sem, kf_exp.at(b, u + 1))
                    mm = nc.tensor.matmul(pa[u][:, 0:4 * T], orf[:, u * 128:u * 128 + 128],
                                          qk[:, 0].rearrange("p t n -> p (t n)"), start=True, stop=True)
                    mm.then_inc(qf_mm.sem, 1)

            def a_kv(b, p):
                if isinstance(b, int) and b == 0:
                    pe.wait_ge(vector_presets, VECTOR_PRESETS)
                pe.wait_ge(kf_ready.sem, kf_ready.at(b))
                pe.wait_ge(qf_exp.sem, qf_exp.at(b, 1))
                for h in range(H):
                    r, c = 64 * (h % 2), h * V1
                    mm = nc.tensor.matmul(pa[0][r:r + 64, c:c + V1], kf[0:T, h * M:(h + 1) * M], v1[:, h],
                                          start=True, stop=True)
                mm.then_inc(kv_mm.sem, 1)

            def a_read(b, p):
                if isinstance(b, int) and b == 0:
                    pe.wait_ge(presets, PRESETS)
                pe.wait_ge(bd_ready.sem, bd_ready.at(b))
                pe.wait_ge(qf_ready.sem, qf_ready.at(b))
                for j in range(PAIRS):
                    r, c = 64 * (j % 2), j // 2
                    mm = nc.tensor.matmul(pa[1][r:r + 64, c * T:(c + 1) * T], bd[:, j], qf[:, j % 2, j // 2],
                                          start=True, stop=True)
                mm.then_inc(ao_mm.sem, 1)

            def a_normalize(b, p):
                if isinstance(b, int) and b == 0:
                    pe.wait_ge(consts_in, 16)
                pe.wait_ge(ao_ready.sem, ao_ready.at(b))
                for c in range(4):
                    mm = nc.tensor.transpose(pa[0][0:T, c * 128:c * 128 + 128], ao[:, c], idn)
                mm.then_inc(aot_mm.sem, 1)

            def a_turn(b, p):
                pe.wait_ge(an_ready.sem, an_ready.at(b))
                for k in range(KT):
                    mm = nc.tensor.transpose(pa[1][:, k * T:(k + 1) * T], an[:, k * 128:k * 128 + 128], idn[0:T, 0:T])
                mm.then_inc(ant_mm.sem, 1)

            def a_output(b, p):
                if isinstance(b, int) and b == 0:
                    pe.wait_ge(tail_weights_in, 16)
                pe.wait_ge(ant_ready.sem, ant_ready.at(b))
                for k in range(KT):
                    mm = nc.tensor.matmul(pa[0][0:T, 0:D], ant[:, k], wo[:, k], start=(k == 0), stop=(k == KT - 1))
                mm.then_inc(wo_mm.sem, 1)

            def a_pack(b, p):
                pe.wait_ge(qs_ready.sem, qs_ready.at(b))
                if isinstance(b, int) and b == 0:
                    pe.wait_ge(ident_ready, 1)
                for half in range(2):
                    dst = pa[half][:, 0:PAIRS // 2 * T // 2].bitcast(F16)
                    for g in range(PAIRS // 2):
                        mm = nc.tensor.transpose(dst[:, g * T:(g + 1) * T], qs[:, half * PAIRS // 2 + g], idh[0:T, 0:T])
                    mm.then_inc(qp_mm.sem, 1)

            def b_max(n):
                def step(b, p):
                    if n == 0:
                        pe.wait_ge(qp_ready.sem, qp_ready.at(b))
                        pe.wait_ge(kp_low.sem, kp_low.at(b))
                        pe.wait_ge(mrow_in.sem[p], mrow_in.at(b, p))
                        if isinstance(b, int) and b == 0:
                            pe.wait_ge(shift_row, 1)
                        pe.wait_ge(lg_ready.sem, lg_ready.back(b))
                    for h in (2 * n, 2 * n + 1):
                        if h == 1:
                            pe.wait_ge(x2l_ready.sem, x2l_ready.back(b))
                        elif h >= 2:
                            pe.wait_ge(max_ready.sem, max_ready.at(b, h - 1))
                        nc.tensor.matmul(psc[h % 2][0:T, 0:S2], qp[:, p, h // 2, h % 2], kp[:, p, h // 2],
                                         start=True, stop=True).then_inc(max_mm.sem, 1)
                return step

            def b_shift(b, p):
                pe.wait_ge(nm_ready.sem, nm_ready.at(b))
                for n in range(2):
                    dst = psc[n][:, 0:8 * T // 2].bitcast(F16)
                    for h in range(8):
                        mm = nc.tensor.transpose(dst[96:97, h * T:(h + 1) * T], nm[:, 8 * n + h:8 * n + h + 1],
                                                 idh[0:T, 0:T], tile_position=(0, 96))
                    mm.then_inc(nmt_mm.sem, 1)

            def values(b, p, u):
                q, c = u // NC, u % NC
                pe.wait_ge(p_ready.sem, p_ready.at(b, u + 1))
                if u == 0:
                    pe.wait_ge(v_in.sem[p], v_in.at(b, p))
                    pe.wait_ge(bo2_ready.sem, bo2_ready.back(b))
                for j in range(4):
                    mm = nc.tensor.matmul(ppv[32 * j:32 * j + V1, q * T:(q + 1) * T], vx[:, p, c, 4 * q + j],
                                          pr[:, u % NP, j * T:(j + 1) * T], start=(c == 0), stop=(c == NC - 1))
                mm.then_inc(pv_mm.sem, 1)

            def b_unit(u):
                def step(b, p):
                    q, c = u // NC, u % NC
                    if u < 2:
                        pe.wait_ge(nmrow_ready.sem, nmrow_ready.at(b))
                    else:
                        pe.wait_ge(p_ready.sem, p_ready.at(b, u - 1))
                    for n in range(2):
                        mm = nc.tensor.matmul(psc[u % 2][0:CH, n * 2 * T:(n + 1) * 2 * T],
                                              kp[:, p, 2 * q + n, c * CH:(c + 1) * CH],
                                              qp[:, p, 2 * q + n].rearrange("p h t -> p (h t)"), start=True, stop=True)
                    mm.then_inc(s_mm.sem, 1)
                    if u >= 1:
                        values(b, p, u - 1)
                return step

            def b_gather(b, p):
                values(b, p, QUADS * NC - 1)

            def b_normalize(b, p):
                pe.wait_ge(bo2_ready.sem, bo2_ready.at(b))
                for c in range(4):
                    mm = nc.tensor.transpose(psc[0][0:T, c * 128:c * 128 + 128], bo2[:, c], idn)
                mm.then_inc(bot_mm.sem, 1)

            def b_turn(b, p):
                pe.wait_ge(bn_ready.sem, bn_ready.at(b))
                for k in range(KT):
                    mm = nc.tensor.transpose(psc[1][:, k * T:(k + 1) * T], bn[:, k * 128:k * 128 + 128], idn[0:T, 0:T])
                mm.then_inc(bnt_mm.sem, 1)

            def b_output(b, p):
                pe.wait_ge(bnt_ready.sem, bnt_ready.at(b))
                for k in range(KT):
                    mm = nc.tensor.matmul(psc[0][0:T, 0:D], bnt[:, k], wfc[:, k], start=(k == 0), stop=(k == KT - 1))
                mm.then_inc(fc_mm.sem, 1)

            def b_turn_x(b, p):
                pe.wait_ge(x2_ready.sem, x2_ready.at(b))
                for k in range(KT):
                    mm = nc.tensor.transpose(psc[1][:, k * T:(k + 1) * T], x2[:, p, k * 128:k * 128 + 128], idn[0:T, 0:T])
                mm.then_inc(x2t_mm.sem, 1)

            def b_logits(b, p):
                pe.wait_ge(x2l_ready.sem, x2l_ready.at(b))
                if isinstance(b, int) and b == 0:
                    pe.wait_ge(low_weights, 1)
                n = 0
                for xs in (x2l, x2h):
                    for ws in (wr_l, wr_h):
                        for k in range(KT):
                            mm = nc.tensor.matmul(psc[0][0:T, 0:E], xs[:, p, k], ws[:, k], start=(n == 0), stop=(n == 4 * KT - 1))
                            n += 1
                mm.then_inc(lg_mm.sem, 1)

            def c_up(e, half):
                def step(b, p):
                    if half == 0:
                        if e == 0:
                            pe.wait_ge(x2l_ready.sem, x2l_ready.at(b))
                            pe.wait_ge(low_weights, 1 + E)
                        if e >= 2:
                            pe.wait_ge(hd_ready.sem, hd_ready.at(b, e - 1))
                        else:
                            pe.wait_ge(hd_ready.sem, hd_ready.back(b))
                    for m in (2 * half, 2 * half + 1):
                        n = 0
                        for ws, xs in ((wex_l, x2h), (wex_h, x2l), (wex_h, x2h)):
                            for k in range(KT):
                                c = k * 2 * DE + m * 128
                                mm = nc.tensor.matmul(pu[e % 2][:, m * T:(m + 1) * T], ws[:, e, c:c + 128],
                                                      xs[:, p, k], start=(n == 0), stop=(n == 3 * KT - 1))
                                n += 1
                    if half:
                        mm.then_inc(up_mm.sem, 1)
                return step

            def c_down(e):
                def step(b, p):
                    pe.wait_ge(hd_low.sem, hd_low.at(b, e + 1))
                    if e == 0:
                        pe.wait_ge(acc_ready.sem, acc_ready.back(b))
                    else:
                        pe.wait_ge(acc_ready.sem, acc_ready.at(b, e))
                    n = 0
                    for hs, ws in ((hd_l, wex_h), (hd_h, wex_l), (hd_h, wex_h)):
                        for k in range(2):
                            c = KT * 2 * DE + k * D
                            mm = nc.tensor.matmul(pd[0:T, 0:D], hs[:, e % NH, k * T:(k + 1) * T], ws[:, e, c:c + D],
                                                  start=(n == 0), stop=(n == 5))
                            n += 1
                    mm.then_inc(dn_mm.sem, 1)
                return step

            pipeline(pe, {
                ("A", "qk"): a_qk, ("A", "v"): a_v, ("A", "k_features"): a_k_features, ("A", "q_features"): a_q_features,
                ("A", "kv"): a_kv, ("A", "read"): a_read, ("A", "normalize"): a_normalize, ("A", "turn"): a_turn,
                ("A", "output"): a_output, ("A", "pack"): a_pack,
                ("B", "shift"): b_shift, ("B", "gather"): b_gather, ("B", "normalize"): b_normalize, ("B", "turn"): b_turn,
                ("B", "output"): b_output, ("B", "turn_x"): b_turn_x, ("B", "logits"): b_logits,
            } | {("B", f"max{n}"): b_max(n) for n in range(H // 2)} | {("B", f"unit{u}"): b_unit(u) for u in range(QUADS * NC)}
              | {("C", f"up_{'ab'[h]}{e}"): c_up(e, h) for e in range(E) for h in range(2)}
              | {("C", f"down{e}"): c_down(e) for e in range(E)})

        @block.scalar
        def _(act):
            def a_qk(b, p):
                act.wait_ge(qk_mm.sem, qk_mm.at(b))
                act.wait_ge(qf_mm.sem, qf_mm.back(b))
                for n in range(2):
                    for c in range(KT):
                        col = n * KT + c
                        last = nc.scalar.activation(qk[0:64, n, 2 * c + 1], pa[0][64:128, col * T:(col + 1) * T],
                                                    ACT.Identity, bias=bqk[64:128, col:col + 1])
                last.then_inc(qk_ready.sem, 1)
                act.wait_ge(qk_ready.sem, qk_ready.at(b))
                nc.scalar.activation(qk[64:128].rearrange("p n t m -> p (n t m)"), qk[0:64].rearrange("p n t m -> p (n t m)"),
                                     ACT.Square).then_inc(squares.sem, 1)

            def a_high(n):
                def step(b, p):
                    act.wait_ge(ctx_in.sem[p], ctx_in.at(b, p))
                    act.wait_ge(s_mm.sem, s_mm.back(b, 2))
                    g = slice(4 * n, 4 * n + 4)
                    nc.scalar.copy(kp[0:96, p, g].rearrange("p g s -> p (g s)"),
                                   kc[:, p, g].rearrange("p g s -> p (g s)")).then_inc(kp_high.sem, 1)
                return step

            def a_k_features(b, p):
                for i in range(2):
                    act.wait_ge(kf_mm.sem, kf_mm.at(b, i + 1))
                    act.wait_ge(kv_mm.sem, kv_mm.back(b))
                    nc.scalar.activation(kf[0:T, i * 512:i * 512 + 512], pa[i][0:T, 0:512], ACT.Exp,
                                         scale=0.5).then_inc(kf_exp.sem, 1)

            def a_q_features(b, p):
                for u in range(2):
                    act.wait_ge(qf_mm.sem, qf_mm.at(b, u + 1))
                    act.wait_ge(ao_mm.sem, ao_mm.back(b))
                    nc.scalar.activation(qf[:, u].rearrange("p t n -> p (t n)"), pa[u][:, 0:4 * T], ACT.Exp,
                                         scale=0.5).then_inc(qf_exp.sem, 1)

            def a_kv(b, p):
                act.wait_ge(kv_mm.sem, kv_mm.at(b))
                act.wait_ge(ao_mm.sem, ao_mm.back(b))
                kv = pa[0][:, 0:PAIRS * 2 * V1].rearrange("p (j d) -> p j d", d=2 * V1)
                nc.scalar.copy(bd[0:64, :, 0:V1], kv[0:64, :, 0:V1]).then_inc(bd_ready.sem, 1)
                nc.scalar.copy(bd[64:128, :, V1:2 * V1], kv[64:128, :, V1:2 * V1]).then_inc(bd_ready.sem, 1)

            def a_read(b, p):
                act.wait_ge(ao_mm.sem, ao_mm.at(b))
                act.wait_ge(aot_mm.sem, aot_mm.back(b))
                nc.scalar.copy(ao[:].rearrange("p c t -> p (c t)"), pa[1][:, 0:4 * T]).then_inc(ao_ready.sem, 1)

            def a_turn(b, p):
                act.wait_ge(ant_mm.sem, ant_mm.at(b))
                act.wait_ge(wo_mm.sem, wo_mm.back(b))
                nc.scalar.copy(ant[:].rearrange("p k t -> p (k t)"), pa[1][:, 0:KT * T]).then_inc(ant_ready.sem, 1)

            def a_pack(b, p):
                act.wait_ge(qp_mm.sem, qp_mm.at(b))
                act.wait_ge(s_mm.sem, s_mm.back(b, 2))
                src = pa[1][:, 0:PAIRS // 2 * T // 2].bitcast(F16).rearrange("p (g t) -> p g t", g=PAIRS // 2)
                for h in range(2):
                    nc.scalar.activation(qp[:, p, PAIRS // 2:PAIRS, h], src, ACT.Copy, scale=pick[:, h:h + 1]).then_inc(qp_ready.sem, 1)

            def b_shift(b, p):
                for n in range(2):
                    act.wait_ge(nmt_mm.sem, nmt_mm.at(b, n + 1))
                    src = psc[n][:, 0:8 * T // 2].bitcast(F16)
                    nc.scalar.copy(qp[96:97, p, 4 * n:4 * n + 4].rearrange("p g h t -> p (g h t)"),
                                   src[96:97, 0:8 * T]).then_inc(nmrow_ready.sem, 1)

            def b_unit(u):
                def step(b, p):
                    act.wait_ge(s_mm.sem, s_mm.at(b, u + 1))
                    if u >= NP:
                        act.wait_ge(pv_mm.sem, pv_mm.at(b, u - NP + 1))
                    else:
                        act.wait_ge(pv_mm.sem, pv_mm.back(b))
                    nc.scalar.activation(pr[:, u % NP], psc[u % 2][0:CH, 0:4 * T], ACT.Exp,
                                         scale=1.0 / 16.0).then_inc(p_ready.sem, 1)
                return step

            def b_gather(b, p):
                act.wait_ge(pv_mm.sem, pv_mm.at(b))
                act.wait_ge(bot_mm.sem, bot_mm.back(b))
                nc.scalar.copy(bo2[:].rearrange("p c t -> p (c t)"), ppv[:, 0:4 * T]).then_inc(bo2_ready.sem, 1)

            def b_turn(b, p):
                act.wait_ge(bnt_mm.sem, bnt_mm.at(b))
                act.wait_ge(fc_mm.sem, fc_mm.back(b))
                nc.scalar.copy(bnt[:].rearrange("p k t -> p (k t)"), psc[1][:, 0:KT * T]).then_inc(bnt_ready.sem, 1)

            def b_turn_x(b, p):
                act.wait_ge(x2t_mm.sem, x2t_mm.at(b))
                act.wait_ge(up_mm.sem, up_mm.back(b, 2))
                nc.scalar.copy(x2h[:, p].rearrange("p k t -> p (k t)"), psc[1][:, 0:KT * T]).then_inc(x2h_ready.sem, 1)

            def c_route2(b, p):
                act.wait_ge(route.sem, route.at(b, 2))
                nc.scalar.activation(ee[:], m8[:, 0:2], ACT.Exp, bias=nm0[:, 0:1]).then_inc(ee_ready.sem, 1)

            def tanh(e):
                def step(b, p):
                    act.wait_ge(up_mm.sem, up_mm.at(b, e + 1))
                    if e >= 2:
                        act.wait_ge(w1_ready.sem, w1_ready.at(b, e - 1))
                    else:
                        act.wait_ge(w1_ready.sem, w1_ready.back(b))
                    nc.scalar.activation(th[:, e % 2], pu[e % 2][:, 0:2 * T], ACT.Tanh, scale=0.5 / WSCALE).then_inc(th_ready.sem, 1)
                return step

            def high(e):
                def step(b, p):
                    act.wait_ge(hd_ready.sem, hd_ready.at(b, e + 1))
                    if e >= NH:
                        act.wait_ge(dn_mm.sem, dn_mm.at(b, e - NH + 1))
                    else:
                        act.wait_ge(dn_mm.sem, dn_mm.back(b))
                    nc.scalar.copy(hd_h[:, e % NH], hd[:, e % 2]).then_inc(hd_high.sem, 1)
                return step

            def c_store(b, p):
                act.wait_ge(y_ready.sem, y_ready.at(b))
                act.dma_start(out[bass.ds(b, 1)].rearrange("o t d -> (o t) d"), yo[:, p]).then_inc(y_out.sem[p], 16)

            def w_split(e):
                def step(b, p):
                    if e == 0:
                        act.wait_ge(tail_weights_in, 16)
                        nc.scalar.mul(wr_h[:].rearrange("p k e -> p (k e)"), wr.rearrange("p k e -> p (k e)"),
                                      WSCALE).then_inc(high_weights, 1)
                    act.wait_ge(experts_in[e], 16)
                    nc.scalar.mul(wex_h[:, e], wex[:, e % NX], WSCALE).then_inc(high_weights, 1)
                return step

            act.wait_ge(presets, PRESETS)
            act.wait_ge(consts_in, 16)
            nc.scalar.copy(idh[:], idn).then_inc(ident_ready, 1)
            pipeline(act, {
                ("A", "qk"): a_qk, ("A", "high0"): a_high(0), ("A", "high1"): a_high(1), ("A", "k_features"): a_k_features,
                ("A", "q_features"): a_q_features, ("A", "kv"): a_kv, ("A", "read"): a_read, ("A", "turn"): a_turn,
                ("A", "pack"): a_pack, ("B", "shift"): b_shift, ("B", "gather"): b_gather, ("B", "turn"): b_turn, ("B", "turn_x"): b_turn_x,
                ("C", "route2"): c_route2, ("C", "store"): c_store,
            } | {("W", str(e)): w_split(e) for e in range(E)}
              | {("B", f"unit{u}"): b_unit(u) for u in range(QUADS * NC)}
              | {("C", f"up_b{e}"): tanh(e) for e in range(E)} | {("C", f"split{e}"): high(e) for e in range(E)})

        @block.vector
        def _(dve):
            def statistics(b, src, stats, mean_var, st, mv):
                nc.vector.bn_stats(stats[:], src).then_inc(st.sem, 1)
                hold(dve, st.sem, st.at(b))
                nc.vector.bn_aggr(mean_var[0:T], stats[:]).then_inc(mv.sem, 1)

            def normalized(b, src, mean_var, rs, rsr, dst, done):
                dve.wait_ge(rsr.sem, rsr.at(b))
                nc.vector.tensor_scalar(dst, src, mean_var[0:T, 0:1], rs[0:T, 1:2], ALU.subtract, ALU.mult).then_inc(done.sem, 1)

            def a_qk(b, p):
                dve.wait_ge(qk_mm.sem, qk_mm.at(b))
                dve.wait_ge(qf_mm.sem, qf_mm.back(b))
                dst = qk[0:64].rearrange("p n (c w) t -> p (n c) w t", w=2)
                nc.vector.tensor_tensor(dst[:, :, 0], pa[0][0:64, 0:4 * T].rearrange("p (c t) -> p c t", c=4),
                                        bqk[0:64].unsqueeze(2).to_broadcast([64, 4, T]), ALU.add).then_inc(qk_ready.sem, 1)

            def a_v(b, p):
                if isinstance(b, int) and b == 0:
                    dve.wait_ge(v_weights_in, 16)
                dve.wait_ge(v_mm.sem, v_mm.at(b))
                dve.wait_ge(kv_mm.sem, kv_mm.back(b))
                nc.vector.tensor_tensor(v1[:, :, 0:DH], pa[1][0:T, 0:D].rearrange("p (h d) -> p h d", h=H),
                                        bv[0:T].rearrange("p (h d) -> p h d", h=H), ALU.add).then_inc(v_ready.sem, 1)

            def a_low(n):
                def step(b, p):
                    dve.wait_ge(kp_high.sem, kp_high.at(b, n // 2 + 1))
                    g = slice(2 * n, 2 * n + 2)
                    nc.vector.tensor_tensor(kp[64:96, p, g], kc[64:96, p, g], kp[64:96, p, g],
                                            ALU.subtract).then_inc(kp_low.sem, 1)
                return step

            def a_normalize(b, p):
                dve.wait_ge(aot_mm.sem, aot_mm.at(b))
                sums = pa[0][0:T, 0:512].rearrange("p (j r) -> p j r", j=PAIRS)[:, :, 0:2 * V1].rearrange(
                    "p j (h d) -> p j h d", h=2)
                nc.vector.reciprocal(rda[:].rearrange("p (j h) -> p j h", h=2), sums[:, :, :, DH]).then_inc(rda_ready.sem, 1)
                dve.wait_ge(rda_ready.sem, rda_ready.at(b))
                dve.wait_ge(ant_mm.sem, ant_mm.back(b))
                nc.vector.tensor_tensor(an[:].rearrange("p (j h d) -> p j h d", j=PAIRS, h=2), sums[:, :, :, 0:DH],
                                        rda[:].rearrange("p (j h) -> p j h", h=2).unsqueeze(3).to_broadcast([T, PAIRS, 2, DH]),
                                        ALU.mult).then_inc(an_ready.sem, 1)

            def a_output(b, p):
                dve.wait_ge(wo_mm.sem, wo_mm.at(b))
                dve.wait_ge(xbo_ready.sem, xbo_ready.at(b))
                dve.wait_ge(x1_ready.sem, x1_ready.back(b))
                nc.vector.tensor_tensor(ra[:], pa[0][0:T, 0:D], xbo[0:T], ALU.add).then_inc(ra_ready.sem, 1)
                dve.wait_ge(ra_ready.sem, ra_ready.at(b))
                statistics(b, ra[:], sta, mva, sta_ready, mva_ready)

            def a_apply(b, p):
                normalized(b, ra[:], mva, rsa, rsa_ready, x1[0:T, p], x1_ready)
                x1_v = x1[0:T, p].rearrange("p (g r) -> p g r", g=PAIRS)
                dve.wait_ge(x1_ready.sem, x1_ready.at(b))
                dve.wait_ge(qp_mm.sem, qp_mm.back(b))
                nc.vector.tensor_copy(
                    qs[:, :, 0:128].rearrange("p g (n r) -> p g n r", n=2)[:, :, :, 0:32],
                    x1_v.unsqueeze(2).to_broadcast([T, PAIRS, 2, 32])).then_inc(qs_ready.sem, 1)
                dve.wait_ge(qs_ready.sem, qs_ready.at(b, 1))
                nc.vector.tensor_tensor(qs[:, :, 32:64], x1_v, qs[:, :, 0:32], ALU.subtract).then_inc(qs_ready.sem, 1)

            def a_pack(b, p):
                dve.wait_ge(qp_mm.sem, qp_mm.at(b, 1))
                dve.wait_ge(s_mm.sem, s_mm.back(b, 2))
                src = pa[0][:, 0:PAIRS // 2 * T // 2].bitcast(F16).rearrange("p (g t) -> p g t", g=PAIRS // 2)
                for h in range(2):
                    nc.vector.tensor_scalar(qp[:, p, 0:PAIRS // 2, h], src, pick[:, h:h + 1], None, ALU.mult).then_inc(qp_ready.sem, 1)

            def b_max(n):
                def step(b, p):
                    for h in (2 * n, 2 * n + 1):
                        dve.wait_ge(max_mm.sem, max_mm.at(b, h + 1))
                        if h == 0:
                            dve.wait_ge(nm_ready.sem, nm_ready.back(b))
                        nc.vector.tensor_reduce(mx[:, h:h + 1], psc[h % 2][0:T, 0:S2], AX_X, ALU.max).then_inc(max_ready.sem, 1)
                return step

            def b_shift(b, p):
                dve.wait_ge(max_ready.sem, max_ready.at(b))
                dve.wait_ge(nmt_mm.sem, nmt_mm.back(b))
                nc.vector.tensor_scalar(nm[:], mx[:], -1.0 / SHIFT, None, ALU.mult).then_inc(nm_ready.sem, 1)

            def b_normalize(b, p):
                dve.wait_ge(bot_mm.sem, bot_mm.at(b))
                sums = psc[0][0:T, 0:512].rearrange("p (h r) -> p h r", h=H)
                nc.vector.reciprocal(rdb[:].unsqueeze(2), sums[:, :, DH:V1]).then_inc(rdb_ready.sem, 1)
                dve.wait_ge(rdb_ready.sem, rdb_ready.at(b))
                dve.wait_ge(bnt_mm.sem, bnt_mm.back(b))
                nc.vector.tensor_tensor(bn[:].rearrange("p (h d) -> p h d", h=H), sums[:, :, 0:DH],
                                        rdb[:].unsqueeze(2).to_broadcast([T, H, DH]), ALU.mult).then_inc(bn_ready.sem, 1)

            def b_output(b, p):
                dve.wait_ge(fc_mm.sem, fc_mm.at(b))
                dve.wait_ge(x1b_ready.sem, x1b_ready.at(b))
                dve.wait_ge(x2_ready.sem, x2_ready.back(b))
                nc.vector.tensor_tensor(rb[:], psc[0][0:T, 0:D], x1b[0:T], ALU.add).then_inc(rb_ready.sem, 1)
                dve.wait_ge(rb_ready.sem, rb_ready.at(b))
                statistics(b, rb[:], stb, mvb, stb_ready, mvb_ready)

            def b_apply(b, p):
                normalized(b, rb[:], mvb, rsb, rsb_ready, x2[:, p], x2_ready)

            def b_turn_x(b, p):
                dve.wait_ge(x2h_ready.sem, x2h_ready.at(b))
                nc.vector.tensor_tensor(x2l[:, p].rearrange("p k t -> p (k t)"), psc[1][:, 0:KT * T],
                                        x2h[:, p].rearrange("p k t -> p (k t)"), ALU.subtract).then_inc(x2l_ready.sem, 1)

            def b_logits(b, p):
                dve.wait_ge(lg_mm.sem, lg_mm.at(b))
                dve.wait_ge(route.sem, route.back(b))
                nc.vector.tensor_scalar(lg[:], psc[0][0:T, 0:E], 1.0 / WSCALE, None, ALU.mult).then_inc(lg_ready.sem, 1)

            def c_route1(b, p):
                hold(dve, lg_ready.sem, lg_ready.at(b))
                nc.vector.max(m8[:], lg[:]).then_inc(route.sem, 1)

            def c_route2(b, p):
                dve.wait_ge(route.sem, route.at(b, 1))
                nc.vector.tensor_scalar(nm0[:], m8[:, 0:1], -1.0, None, ALU.mult).then_inc(route.sem, 1)
                nc.vector.max_index(i8[:], m8[:], lg[:]).then_inc(route.sem, 1)

            def c_route3(b, p):
                dve.wait_ge(route.sem, route.at(b, 3))
                nc.vector.tensor_copy(i8f[:], i8[:, 0:2]).then_inc(route.sem, 1)
                dve.wait_ge(ee_ready.sem, ee_ready.at(b))
                nc.vector.tensor_tensor(es[:], ee[:, 0:1], ee[:, 1:2], ALU.add).then_inc(route.sem, 1)

            def c_route4(b, p):
                dve.wait_ge(route.sem, route.at(b, 5))
                nc.vector.reciprocal(er[:], es[:]).then_inc(route.sem, 1)

            def c_route5(b, p):
                dve.wait_ge(route.sem, route.at(b, 6))
                nc.vector.tensor_scalar(gg[:], ee[:], er[:, 0:1], 0.5 / WSCALE, ALU.mult, ALU.mult).then_inc(route.sem, 1)

            def c_route6(b, p):
                dve.wait_ge(route.sem, route.at(b, 7))
                for n in range(2):
                    last = nc.vector.tensor_scalar(g01[:, n], pick[0:T, 2:2 + E], i8f[:, n:n + 1], gg[:, n:n + 1],
                                                   ALU.is_equal, ALU.mult)
                last.then_inc(route.sem, 1)

            def c_route7(b, p):
                dve.wait_ge(route.sem, route.at(b, 8))
                nc.vector.tensor_tensor(gate[:, p], g01[:, 0], g01[:, 1], ALU.add).then_inc(gate_ready.sem, 1)

            def gated(e):
                def step(b, p):
                    dve.wait_ge(dn_mm.sem, dn_mm.at(b, e + 1))
                    if e == 0:
                        dve.wait_ge(gate_ready.sem, gate_ready.at(b))
                        dve.wait_ge(y_ready.sem, y_ready.back(b))
                        prev = x2[:, p]
                    else:
                        dve.wait_ge(acc_ready.sem, acc_ready.at(b, e))
                        prev = acc[:, (e - 1) % 2]
                    nc.vector.scalar_tensor_tensor(out=acc[:, e % 2], in0=pd[0:T, 0:D], scalar=gate[:, p, e:e + 1], in1=prev,
                                                   op0=ALU.mult, op1=ALU.add).then_inc(acc_ready.sem, 1)
                return step

            def hidden(e):
                def step(b, p):
                    dve.wait_ge(th_ready.sem, th_ready.at(b, e + 1))
                    if e >= 2:
                        dve.wait_ge(hd_ready.sem, hd_ready.at(b, e - 1))
                    else:
                        dve.wait_ge(hd_ready.sem, hd_ready.back(b))
                    nc.vector.scalar_tensor_tensor(out=w1[:, e % 2], in0=th[:, e % 2], scalar=1.0, in1=pu[e % 2][:, 0:2 * T],
                                                   op0=ALU.add, op1=ALU.mult).then_inc(w1_ready.sem, 1)
                    dve.wait_ge(w1_ready.sem, w1_ready.at(b, e + 1))
                    if e >= 2:
                        dve.wait_ge(hd_low.sem, hd_low.at(b, e - 1))
                    else:
                        dve.wait_ge(hd_low.sem, hd_low.back(b))
                    nc.vector.scalar_tensor_tensor(out=hd[:, e % 2], in0=w1[:, e % 2], scalar=1.0 / WSCALE ** 2,
                                                   in1=pu[e % 2][:, 2 * T:4 * T], op0=ALU.mult, op1=ALU.mult).then_inc(hd_ready.sem, 1)
                return step

            def c_finish(b, p):
                gated(E - 1)(b, p)
                dve.wait_ge(acc_ready.sem, acc_ready.at(b))
                statistics(b, acc[:, (E - 1) % 2], stc, mvc, stc_ready, mvc_ready)

            def c_store(b, p):
                dve.wait_ge(y_out.sem[p], y_out.back(b, p))
                normalized(b, acc[:, (E - 1) % 2], mvc, rsc, rsc_ready, yo[:, p], y_ready)

            def w_split(e):
                def step(b, p):
                    if e == 0:
                        dve.wait_ge(high_weights, 1)
                        nc.vector.scalar_tensor_tensor(out=wr_l[:].rearrange("p k e -> p (k e)"),
                                                       in0=wr.rearrange("p k e -> p (k e)"), scalar=WSCALE,
                                                       in1=wr_h[:].rearrange("p k e -> p (k e)"),
                                                       op0=ALU.mult, op1=ALU.subtract).then_inc(low_weights, 1)
                    dve.wait_ge(high_weights, e + 2)
                    nc.vector.scalar_tensor_tensor(out=wex_l[:, e], in0=wex[:, e % NX], scalar=WSCALE, in1=wex_h[:, e],
                                                   op0=ALU.mult, op1=ALU.subtract).then_inc(low_weights, 1)
                return step

            nc.vector.memset(kp_all[96:128].bitcast(F32), 0.0).then_inc(vector_presets, 1)
            nc.vector.memset(ppv[:], 0.0).then_inc(vector_presets, 1)
            nc.vector.memset(v1[:, :, DH:V1], 1.0).then_inc(vector_presets, 1)
            dve.wait_ge(mask_in, 16)
            nc.vector.tensor_scalar(mask_h[:], mask_i[:], 0.0, -BIG, ALU.is_equal, ALU.mult).then_inc(mask_ready, 1)
            dve.wait_ge(presets, PRESETS)
            dve.wait_ge(consts_in, 16)
            pipeline(dve, {
                ("A", "qk"): a_qk, ("A", "v"): a_v, ("A", "normalize"): a_normalize, ("A", "output"): a_output,
                ("A", "apply"): a_apply, ("A", "pack"): a_pack,
                ("B", "shift"): b_shift, ("B", "normalize"): b_normalize, ("B", "output"): b_output, ("B", "apply"): b_apply,
                ("B", "turn_x"): b_turn_x, ("B", "logits"): b_logits,
                ("C", "route1"): c_route1, ("C", "route2"): c_route2, ("C", "route3"): c_route3, ("C", "route4"): c_route4,
                ("C", "route5"): c_route5, ("C", "route6"): c_route6, ("C", "route7"): c_route7, ("C", "finish"): c_finish, ("C", "store"): c_store,
            } | {("W", str(e)): w_split(e) for e in range(E)}
              | {("A", f"low{n}"): a_low(n) for n in range(4)} | {("B", f"max{n}"): b_max(n) for n in range(H // 2)}
              | {("C", f"hidden{e}"): hidden(e) for e in range(E)} | {("C", f"gated{e}"): gated(e) for e in range(E - 1)})

        @block.gpsimd
        def _(pool):
            def inverse_root(b, mv, mean_var, rs, rsr):
                hold(pool, mv.sem, mv.at(b))
                nc.gpsimd.tensor_scalar(rs[:, 0:1], mean_var[:, 1:2], LN_EPS, 1.0, ALU.add, ALU.mult).then_inc(rsr.sem, 1)
                pool.wait_ge(rsr.sem, rsr.at(b, 1))
                nc.gpsimd.tensor_tensor(rs[:, 1:2], rs[:, 0:1], pick[:, 2 + E:3 + E], ALU.pow).then_inc(rsr.sem, 1)

            def a_k_features(b, p):
                for i in range(2):
                    hold(pool, kf_exp.sem, kf_exp.at(b, i + 1))
                    nc.gpsimd.tensor_scalar(kf[:, i * 512:i * 512 + 512], kf[:, i * 512:i * 512 + 512], FEATURE_EPS, 1.0,
                                            ALU.add, ALU.mult).then_inc(kf_ready.sem, 1)

            def a_q_features(b, p):
                for u in range(2):
                    hold(pool, qf_exp.sem, qf_exp.at(b, u + 1))
                    nc.gpsimd.tensor_scalar(qf[:, u], qf[:, u], FEATURE_EPS, 1.0, ALU.add, ALU.mult).then_inc(qf_ready.sem, 1)

            def a_kv(b, p):
                pool.wait_ge(x_in.sem[p], x_in.at(b, p))
                pool.wait_ge(ra_ready.sem, ra_ready.back(b))
                if isinstance(b, int) and b == 0:
                    pool.wait_ge(tail_weights_in, 16)
                nc.gpsimd.tensor_tensor(xbo[:], xr[:, p], bo, ALU.add).then_inc(xbo_ready.sem, 1)

            def a_output(b, p):
                inverse_root(b, mva_ready, mva, rsa, rsa_ready)

            def b_shift(b, p):
                pool.wait_ge(x1_ready.sem, x1_ready.at(b))
                pool.wait_ge(rb_ready.sem, rb_ready.back(b))
                nc.gpsimd.tensor_tensor(x1b[:], x1[:, p], bfc, ALU.add).then_inc(x1b_ready.sem, 1)

            def b_output(b, p):
                inverse_root(b, mvb_ready, mvb, rsb, rsb_ready)

            def low(e):
                def step(b, p):
                    pool.wait_ge(hd_high.sem, hd_high.at(b, e + 1))
                    if e >= NH:
                        pool.wait_ge(dn_mm.sem, dn_mm.at(b, e - NH + 1))
                    else:
                        pool.wait_ge(dn_mm.sem, dn_mm.back(b))
                    nc.gpsimd.tensor_tensor(hd_l[:, e % NH], hd[:, e % 2], hd_h[:, e % NH], ALU.subtract).then_inc(hd_low.sem, 1)
                return step

            def c_finish(b, p):
                inverse_root(b, mvc_ready, mvc, rsc, rsc_ready)

            for n, (ap, value) in enumerate((
                    (kf[96:128], 0.0), (x1[96:128], 0.0),
                    (mva[:], 1.0), (mvb[:], 1.0), (mvc[:], 1.0), (bd[:], 0.0), (qs[:, :, 96:128], 0.0),
                    (qs[:, :, 97:98], BIG))):
                if n:
                    pool.wait_ge(presets, n)
                nc.gpsimd.memset(ap, value).then_inc(presets, 1)
            pool.wait_ge(presets, PRESETS)
            pool.wait_ge(vector_presets, VECTOR_PRESETS)
            nc.gpsimd.memset(kp[96:97], SHIFT).then_inc(shift_row, 1)
            pool.wait_ge(shift_row, 1)
            pool.wait_ge(consts_in, 16)
            pipeline(pool, {
                ("A", "k_features"): a_k_features, ("A", "q_features"): a_q_features, ("A", "kv"): a_kv,
                ("A", "output"): a_output, ("B", "shift"): b_shift, ("B", "output"): b_output, ("C", "finish"): c_finish,
            } | {("C", f"split{e}"): low(e) for e in range(E)})


def kernel(**inputs):
    import numpy as np
    import concourse.bacc as bacc
    from concourse.bass_utils import run_bass_kernel_spmd

    f = {n: np.asarray(a) for n, a in inputs.items()}
    x, c = f["x"], f["ctx_1024"]

    def rows128(w):
        return w.reshape(-1, 128, w.shape[-1]).transpose(1, 0, 2)

    def every_token(v):
        return np.broadcast_to(v, (128, D))

    orf_rows = np.zeros((128, 4, M), np.float32)
    for h in range(4):
        orf_rows[h * DH:(h + 1) * DH, h] = f["L0_attn_orf"].T
        orf_rows[64 + h * DH:64 + (h + 1) * DH, h] = -0.25
    picks = np.zeros((128, 2 + E + 1), np.float32)
    for p in range(128):
        picks[p, 0] = p >= 96 or p % 32 < DH
        picks[p, 1] = p >= 96 or p % 32 >= DH
    picks[:, 2:2 + E] = np.arange(E)
    picks[:, 2 + E] = -0.5
    values = np.ones((B, CH, NC, H, V1), np.float32)
    values[..., :DH] = c.reshape(B, NC, CH, H, DH).transpose(0, 2, 1, 3, 4)

    x_both = np.zeros((B, 128, KT * T + D), np.float32)
    x_both[:, :, :KT * T] = x.transpose(0, 2, 1).reshape(B, KT, 128, T).transpose(0, 2, 1, 3).reshape(B, 128, KT * T)
    x_both[:, :T, KT * T:] = x

    def side_by_side(*tensors):
        return np.concatenate([t.reshape(128, -1) for t in tensors], 1)

    arrays = {
        "x_both": x_both,
        "ctx_cols": c.transpose(0, 2, 1).reshape(B, PAIRS, 32, S2).transpose(0, 2, 1, 3),
        "ctx_rows": values,
        "mask": f["mask_Bx1x1xS2_ik0"].reshape(1, B * S2).astype(np.int32),
        "w_q": rows128(f["L0_attn_Wq"].T), "w_k": rows128(f["L0_attn_Wk"].T),
        "w_v": side_by_side(rows128(f["L0_attn_Wv"].T), every_token(f["L0_attn_bv"])),
        "w_tail": side_by_side(rows128(f["L0_attn_Wo"].T), every_token(f["L0_attn_bo"]),
                               rows128(f["L0_xattn_fc_w"].T), every_token(f["L0_xattn_fc_b"]),
                               rows128(f["L0_ffn_router_w"].T)),
        "w_experts": np.concatenate([
            f["L0_ffn_up_proj"].reshape(E, KT, 128, 2 * DE).transpose(2, 0, 1, 3).reshape(128, E, KT * 2 * DE),
            f["L0_ffn_down_proj"].reshape(E, DE // 128, 128, D).transpose(2, 0, 1, 3).reshape(128, E, DE // 128 * D)], 2),
        "consts": side_by_side(f["L0_attn_bq"].reshape(KT, 128).T, f["L0_attn_bk"].reshape(KT, 128).T,
                               orf_rows, np.eye(128, dtype=np.float32), picks),
    }
    nc = bacc.Bacc("TRN2", target_bir_lowering=False, num_devices=1)
    feeds, args = {}, {}
    for name, a in arrays.items():
        a = np.ascontiguousarray(a)
        feeds[f"in_{name}"] = a
        args[name] = nc.dram_tensor(f"in_{name}", a.shape, mybir.dt.from_np(a.dtype), kind="ExternalInput").ap()
    args["out"] = nc.dram_tensor("out", (B, T, D), F32, kind="ExternalOutput").ap()
    build(nc, **args)
    r = run_bass_kernel_spmd(nc, [feeds], core_ids=[0])
    return r.results[0]["out"]
```
